# Optimizing a Trainium2 kernel written in Bass

```python
import numpy as np
import jax
import jax.numpy as jnp

def _softmax(x, axis=-1):
    return jax.nn.softmax(x, axis=axis)

def _gelu(x):
    return jax.nn.gelu(x, approximate=True)

def _silu(x):
    return jax.nn.silu(x)

def _sigmoid(x):
    return jax.nn.sigmoid(x)

def _layernorm(x, axis=-1, eps=1e-05):
    m = jnp.mean(x, axis=axis, keepdims=True)
    v = jnp.var(x, axis=axis, keepdims=True)
    return (x - m) / jnp.sqrt(v + eps)

def _scatter_add(tgt, idx, src, axis=0):
    return tgt.at[idx].add(src)

def _segment_sum(src, seg, n):
    return jax.ops.segment_sum(src, seg, n)
kernel_name = 'mk_xattn_seq_d1_seqx_r4_2746e2'

def setup_inputs(seed: int=0):
    np.random.seed(seed)
    _w = jnp.asarray

    def _rec_inputs():
        import jax
        import jax.numpy as jnp
        _rk = jax.random.key(seed)
        x = -0.0001233 + 1 * jax.random.normal(jax.random.fold_in(_rk, 1), (8, 512, 320), jnp.float32)
        _lenS = 512 - jax.random.randint(jax.random.fold_in(_rk, 7), (8,), 0, max(1, 512 // 4) + 1, jnp.int32)
        _lenS2 = 512 - jax.random.randint(jax.random.fold_in(_rk, 8), (8,), 0, max(1, 512 // 4) + 1, jnp.int32)
        _ctx_768P = jax.random.normal(jax.random.fold_in(_rk, 11), (8, 16, 192), jnp.float32)
        _ctx_768c = jax.random.dirichlet(jax.random.fold_in(_rk, 511), 0.3 * jnp.ones((16,), jnp.float32), (8, 512))
        _ctx_768t = jnp.einsum('bsk,bkd->bsd', _ctx_768c, _ctx_768P)
        _ctx_768t = _ctx_768t * jax.lax.rsqrt(jnp.mean(jnp.square(_ctx_768t)) + 1e-12) * 0.953939
        ctx_768 = 0.00272024 + 0.999456 * (_ctx_768t + 0.3 * jax.random.normal(jax.random.fold_in(_rk, 611), (8, 512, 192), jnp.float32))
        return (x, ctx_768)
    x, ctx_768 = _rec_inputs()

    def _L0_xattn_setup():
        import jax, jax.numpy as jnp
        import numpy as np
        D = 320
        H = 20
        DH = D // H
        CTX = 192
        FF_IN = 4 * D
        EPS = 1e-05

        def _ln(x, g, b):
            m = jnp.mean(x, axis=-1, keepdims=True)
            v = jnp.mean(jnp.square(x - m), axis=-1, keepdims=True)
            return (x - m) * jax.lax.rsqrt(v + EPS) * g + b

        def _attn(x, ctx, wq, wk, wv, wo, bo, heads):
            b, n, _ = x.shape
            j = ctx.shape[1]
            dh = wq.shape[1] // heads
            scale = dh ** (-0.5)
            q = (x @ wq).reshape(b, n, heads, dh).transpose(0, 2, 1, 3)
            k = (ctx @ wk).reshape(b, j, heads, dh).transpose(0, 2, 1, 3)
            v = (ctx @ wv).reshape(b, j, heads, dh).transpose(0, 2, 1, 3)
            sim = jnp.einsum('bhid,bhjd->bhij', q, k) * scale
            a = jax.nn.softmax(sim, axis=-1)
            out = jnp.einsum('bhij,bhjd->bhid', a, v)
            out = out.transpose(0, 2, 1, 3).reshape(b, n, heads * dh)
            return out @ wo + bo
        key = jax.random.key(seed)
        ks = jax.random.split(key, 24)
        r = lambda k, shp, s: jax.random.normal(k, shp, dtype=jnp.float32) * s
        d = {'x': r(ks[0], (8, 256, D), 1.0), 'context': r(ks[1], (8, 77, CTX), 1.0), 'heads': H, 'n1_g': jnp.ones((D,), jnp.float32), 'n1_b': jnp.zeros((D,), jnp.float32), 'q1': r(ks[2], (D, D), D ** (-0.5)), 'k1': r(ks[3], (D, D), D ** (-0.5)), 'v1': r(ks[4], (D, D), D ** (-0.5)), 'o1_w': r(ks[5], (D, D), D ** (-0.5)), 'o1_b': jnp.zeros((D,), jnp.float32), 'n2_g': jnp.ones((D,), jnp.float32), 'n2_b': jnp.zeros((D,), jnp.float32), 'q2': r(ks[6], (D, D), D ** (-0.5)), 'k2': r(ks[7], (CTX, D), CTX ** (-0.5)), 'v2': r(ks[8], (CTX, D), CTX ** (-0.5)), 'o2_w': r(ks[9], (D, D), D ** (-0.5)), 'o2_b': jnp.zeros((D,), jnp.float32), 'n3_g': jnp.ones((D,), jnp.float32), 'n3_b': jnp.zeros((D,), jnp.float32), 'ff_w1': r(ks[10], (D, 2 * FF_IN), D ** (-0.5)), 'ff_b1': jnp.zeros((2 * FF_IN,), jnp.float32), 'ff_w2': r(ks[11], (FF_IN, D), FF_IN ** (-0.5)), 'ff_b2': jnp.zeros((D,), jnp.float32)}
        return d
    _L0_xattn_all = _L0_xattn_setup()
    _L0_xattn_in = {k: v for k, v in _L0_xattn_all.items() if k in ('n1_g', 'n1_b', 'q1', 'k1', 'v1', 'o1_w', 'o1_b', 'n2_g', 'n2_b', 'q2', 'k2', 'v2', 'o2_w', 'o2_b', 'n3_g', 'n3_b', 'ff_w1', 'ff_b1', 'ff_w2', 'ff_b2')}
    del _L0_xattn_all
    return {'x': x, 'ctx_768': ctx_768, 'L0_xattn_n1_g': _L0_xattn_in['n1_g'], 'L0_xattn_n1_b': _L0_xattn_in['n1_b'], 'L0_xattn_q1': _L0_xattn_in['q1'], 'L0_xattn_k1': _L0_xattn_in['k1'], 'L0_xattn_v1': _L0_xattn_in['v1'], 'L0_xattn_o1_w': _L0_xattn_in['o1_w'], 'L0_xattn_o1_b': _L0_xattn_in['o1_b'], 'L0_xattn_n2_g': _L0_xattn_in['n2_g'], 'L0_xattn_n2_b': _L0_xattn_in['n2_b'], 'L0_xattn_q2': _L0_xattn_in['q2'], 'L0_xattn_k2': _L0_xattn_in['k2'], 'L0_xattn_v2': _L0_xattn_in['v2'], 'L0_xattn_o2_w': _L0_xattn_in['o2_w'], 'L0_xattn_o2_b': _L0_xattn_in['o2_b'], 'L0_xattn_n3_g': _L0_xattn_in['n3_g'], 'L0_xattn_n3_b': _L0_xattn_in['n3_b'], 'L0_xattn_ff_w1': _L0_xattn_in['ff_w1'], 'L0_xattn_ff_b1': _L0_xattn_in['ff_b1'], 'L0_xattn_ff_w2': _L0_xattn_in['ff_w2'], 'L0_xattn_ff_b2': _L0_xattn_in['ff_b2']}

def reference(x, ctx_768, L0_xattn_n1_g, L0_xattn_n1_b, L0_xattn_q1, L0_xattn_k1, L0_xattn_v1, L0_xattn_o1_w, L0_xattn_o1_b, L0_xattn_n2_g, L0_xattn_n2_b, L0_xattn_q2, L0_xattn_k2, L0_xattn_v2, L0_xattn_o2_w, L0_xattn_o2_b, L0_xattn_n3_g, L0_xattn_n3_b, L0_xattn_ff_w1, L0_xattn_ff_b1, L0_xattn_ff_w2, L0_xattn_ff_b2):
    import jax
    import jax.numpy as jnp

    def _L0_xattn_ref(x, context, heads, n1_g, n1_b, q1, k1, v1, o1_w, o1_b, n2_g, n2_b, q2, k2, v2, o2_w, o2_b, n3_g, n3_b, ff_w1, ff_b1, ff_w2, ff_b2):
        import jax, jax.numpy as jnp
        import numpy as np
        D = 320
        H = 20
        DH = D // H
        CTX = 192
        FF_IN = 4 * D
        EPS = 1e-05

        def _ln(x, g, b):
            m = jnp.mean(x, axis=-1, keepdims=True)
            v = jnp.mean(jnp.square(x - m), axis=-1, keepdims=True)
            return (x - m) * jax.lax.rsqrt(v + EPS) * g + b

        def _attn(x, ctx, wq, wk, wv, wo, bo, heads):
            b, n, _ = x.shape
            j = ctx.shape[1]
            dh = wq.shape[1] // heads
            scale = dh ** (-0.5)
            q = (x @ wq).reshape(b, n, heads, dh).transpose(0, 2, 1, 3)
            k = (ctx @ wk).reshape(b, j, heads, dh).transpose(0, 2, 1, 3)
            v = (ctx @ wv).reshape(b, j, heads, dh).transpose(0, 2, 1, 3)
            sim = jnp.einsum('bhid,bhjd->bhij', q, k) * scale
            a = jax.nn.softmax(sim, axis=-1)
            out = jnp.einsum('bhij,bhjd->bhid', a, v)
            out = out.transpose(0, 2, 1, 3).reshape(b, n, heads * dh)
            return out @ wo + bo
        h1 = _ln(x, n1_g, n1_b)
        x = _attn(h1, h1, q1, k1, v1, o1_w, o1_b, heads) + x
        h2 = _ln(x, n2_g, n2_b)
        x = _attn(h2, context, q2, k2, v2, o2_w, o2_b, heads) + x
        h3 = _ln(x, n3_g, n3_b)
        proj = h3 @ ff_w1 + ff_b1
        a, g = jnp.split(proj, 2, axis=-1)
        ff = a * jax.nn.gelu(g, approximate=False) @ ff_w2 + ff_b2
        return ff + x
    x = _L0_xattn_ref(x, ctx_768, 20, L0_xattn_n1_g, L0_xattn_n1_b, L0_xattn_q1, L0_xattn_k1, L0_xattn_v1, L0_xattn_o1_w, L0_xattn_o1_b, L0_xattn_n2_g, L0_xattn_n2_b, L0_xattn_q2, L0_xattn_k2, L0_xattn_v2, L0_xattn_o2_w, L0_xattn_o2_b, L0_xattn_n3_g, L0_xattn_n3_b, L0_xattn_ff_w1, L0_xattn_ff_b1, L0_xattn_ff_w2, L0_xattn_ff_b2)
    return x

_drawn_inputs = setup_inputs


def setup_inputs(seed=0):
    import zlib

    import numpy as np

    out = dict(_drawn_inputs(seed))
    spreads = {'L0_xattn_n1_g': (1.0, 0.2),
     'L0_xattn_n1_b': (0.0, 0.1),
     'L0_xattn_o1_b': (0.0, 0.1),
     'L0_xattn_n2_g': (1.0, 0.2),
     'L0_xattn_n2_b': (0.0, 0.347),
     'L0_xattn_o2_b': (0.0, 0.1),
     'L0_xattn_n3_g': (1.0, 0.2),
     'L0_xattn_n3_b': (0.0, 0.1),
     'L0_xattn_ff_b1': (0.0, 0.1),
     'L0_xattn_ff_b2': (0.0, 0.1)}
    factors = {}
    for name, (base, spread) in spreads.items():
        noise = np.random.default_rng([zlib.crc32(name.encode()), seed]).standard_normal(out[name].shape)
        drawn = base * np.exp(spread * noise) if base else spread * noise
        out[name] = jnp.asarray(drawn.astype(out[name].dtype))
    for name, factor in factors.items():
        out[name] = (out[name] * factor).astype(out[name].dtype)
    return out
```

```python
from contextlib import ExitStack

import concourse.bass as bass
from concourse import mybir

F32 = mybir.dt.float32
F32R = mybir.dt.float32r
BF16 = mybir.dt.bfloat16
ALU = mybir.AluOpType
ACT = mybir.ActivationFunctionType
AX_X = mybir.AxisListType.X

P = 128
B, N, D, C = 8, 512, 320, 192
H, DH = 20, 16
F = 1280
EPS = 1e-5
SCALE = DH ** -0.5
NT = N // P
GH = 4
NG = H // GH
UNITS = 2 * B
MAX_ROW = 62
MC = F // P

QA, KA, QKC, QB, KB = range(5)
STACK = [(0, 0, 0), (1, 1, 0), (2, 0, 1)]
RING = [0, 1, 2, 3, 4, 5, 0, 1, 2, 3, 4, 5, 0, 1, 2, 3, 4, 5, 2, 3]

OPS_SELF = ["t0", "t1", "t2", QA, KA, QKC, QB, KB]
OPS_CROSS = ["t0", "t1", "t2", "c0", "c1", QA, KA, QKC, QB, KB]


def ops_of(cross):
    return OPS_CROSS if cross else OPS_SELF


def ops_base(u, cross):
    return 10 * u - 2 * B if cross else 8 * u


def chunk_rows(width, c):
    return min(P, width - c * P)


def wait_apart(eng, sem, value, passed):
    if not isinstance(value, int):
        eng.lower_val(value)
    eng.wait_ge(passed, 1)
    eng.wait_ge(sem, value)


def attention(nc, x, ctx_in, w, x1, x2):
    with ExitStack() as ctx:
        def sb(name, shape, dt=F32):
            return ctx.enter_context(nc.sbuf_tensor(name, shape, dt))

        def sem(name):
            return ctx.enter_context(nc.semaphore(name))

        ps = ctx.enter_context(nc.psum_tensor("ps", [P, 8, 512], F32))
        ST, SM, OB, DB = 0, 4, 6, 7

        xl = sb("xl", [P, NT, D])
        xr = sb("xr", [P, NT, D])
        xn = sb("xn", [P, NT, 3 * P])
        cn = sb("cn", [P, NT, 2 * P])
        mv6 = sb("mv6", [P, NT, 6])
        mv = sb("mv", [P, NT, 2])
        negmean = sb("negmean", [P, NT])
        vareps = sb("vareps", [P, NT])
        rstd = sb("rstd", [P, NT])
        nmr = sb("nmr", [P, NT])
        neghalf = sb("neghalf", [P, NT])
        gb = sb("gb", [P, 2, 3, 2])
        h1 = sb("h1", [P, 3, N], F32R)
        h2 = sb("h2", [P, 2, N], F32R)
        c1 = sb("c1", [P, 2, N], F32R)
        c2 = sb("c2", [P, N], F32R)
        whole = sb("whole", [P, 2, N])
        raw = sb("raw", [P, 2, D])
        wqk1 = sb("wqk1", [P, 3, 5, P], F32R)
        wqk2 = sb("wqk2", [P, 3, 5, P], F32R)
        wv1 = sb("wv1", [P, 3, D], F32R)
        wv2 = sb("wv2", [P, 3, D], F32R)
        wo = sb("wo", [P, NG, D])
        sq = sb("sq", [P, 5, 2, N], F32R)
        qs = sb("qs", [P, H // 2, N], F32R)
        ks = sb("ks", [P, H // 2, N], F32R)
        v = sb("v", [P, NT, H, 32])
        pr = sb("pr", [P, 6, NT, N])
        on = sb("on", [P, NG, N])
        rs = sb("rs", [P, N // 2])
        nm = sb("nm", [P, NT, 2, 2])
        mh = sb("mh", [P, NT, 2, 2, 2], BF16)
        mt = sb("mt", [8, N], F32R)
        ident = sb("ident", [P, P])
        identb = sb("identb", [P, P], BF16)

        const_ready = sem("const_ready")
        ident_zero = sem("ident_zero")
        ident_ready = sem("ident_ready")
        ones_loaded = sem("ones_loaded")
        small_loaded = sem("small_loaded")
        wo_loaded = sem("wo_loaded")
        raw_loaded = [sem("raw_loaded0"), sem("raw_loaded1")]
        raw_split = sem("raw_split")
        w_rounded = sem("w_rounded")
        w_zeroed = sem("w_zeroed")
        xl_loaded = sem("xl_loaded")
        cn_loaded = sem("cn_loaded")
        xr_loaded = sem("xr_loaded")
        x_stored = sem("x_stored")
        stats_raw = sem("stats_raw")
        stats_mv = sem("stats_mv")
        stats_ready = sem("stats_ready")
        rstd_ready = sem("rstd_ready")
        nmr_ready = sem("nmr_ready")
        xn_ready = sem("xn_ready")
        op_ready = sem("op_ready")
        op_evac = sem("op_evac")
        op_split = sem("op_split")
        v_ready = sem("v_ready")
        v_evac = sem("v_evac")
        stacked = [sem("stacked_a"), sem("stacked_b"), sem("stacked_c")]
        smax_ready = sem("smax_ready")
        smax_free = sem("smax_free")
        mh_ready = sem("mh_ready")
        mt_ready = sem("mt_ready")
        mt_evac = sem("mt_evac")
        max_placed = sem("max_placed")
        st_ready = sem("st_ready")
        exp_done = sem("exp_done")
        o_ready = sem("o_ready")
        norm_step = sem("norm_step")
        norm_done = sem("norm_done")
        oproj_ready = sem("oproj_ready")
        res_done = sem("res_done")

        def weight_chunks(cross):
            pre = "2" if cross else "1"
            wide = C if cross else D
            return ([("q" + pre, D, c) for c in range(3)] + [("k" + pre, wide, c) for c in range((wide + P - 1) // P)]
                    + [("v" + pre, wide, c) for c in range((wide + P - 1) // P)])

        def weight_pieces(name, c):
            src = raw[:, 0, :]
            out = []
            if name[0] == "v":
                return [(lambda t: t[0][:, c, :], "v", lambda r: r)]
            first = {"q": 0, "k": 1}[name[0]]
            for tile, h0, nh in ((QA + first, 0, 8), (QB + first, 8, 8), (QKC, 16, 4)):
                def dst(wt, tile=tile, nh=nh):
                    if name == "k2" and nh == 4:
                        a = wt[:, 2, (KA, KB)[c], 64:128]
                    elif nh == 4:
                        a = wt[:, c, tile, 64 * first:64 * first + 64]
                    else:
                        a = wt[:, c, tile, :]
                    return a.rearrange("p (r d h) -> p r d h", r=2, d=DH)

                def src_of(r, h0=h0, nh=nh):
                    return r[:, DH * h0:DH * (h0 + nh)].rearrange("p (h r d) -> p r d h", r=2, d=DH)
                out.append((dst, "qk", src_of))
            return out

        chunks_before = {False: 0, True: len(weight_chunks(False))}
        pieces_before = {False: 0, True: sum(len(weight_pieces(n, c)) for n, _, c in weight_chunks(False))}

        def sp_weights(sp, cross):
            for i, (name, wide, c) in enumerate(weight_chunks(cross), chunks_before[cross]):
                if i >= 2:
                    sp.wait_ge(raw_split, i - 1)
                n = chunk_rows(wide, c)
                for at in range(0, P, n):
                    sp.dma_start(raw[at:at + n, i % 2, :], w[name][c * P:c * P + n, :]).then_inc(raw_loaded[i % 2], 16)

        def raw_full(i):
            plan = weight_chunks(False) + weight_chunks(True)
            return sum(16 * (P // chunk_rows(wide, c)) for _, wide, c in plan[i % 2:i + 1:2])

        def act_weights(act, cross):
            if cross:
                act.wait_ge(v_ready, NT * B)
                act.wait_ge(w_zeroed, 4)
            for i, (name, wide, c) in enumerate(weight_chunks(cross), chunks_before[cross]):
                act.wait_ge(raw_loaded[i % 2], raw_full(i))
                for dst, kind, src in weight_pieces(name, c):
                    to = wv1[:, c, :] if kind == "v" else dst(wqk1)
                    nc.scalar.activation(to, src(raw[:, i % 2, :]), ACT.Copy).then_inc(w_rounded, 1)

        def pool_weights(pool, cross):
            done = pieces_before[cross]
            if cross:
                pool.wait_ge(v_ready, NT * B)
                for wt in (wqk1, wqk2):
                    nc.gpsimd.memset(wt[:, :, QKC, 64:128].bitcast(F32), 0.0).then_inc(w_zeroed, 1)
                    nc.gpsimd.memset(wt[:, 2, 1:5:3, 0:64].bitcast(F32), 0.0).then_inc(w_zeroed, 1)
                pool.wait_ge(w_zeroed, 4)
            for i, (name, wide, c) in enumerate(weight_chunks(cross), chunks_before[cross]):
                pieces = weight_pieces(name, c)
                for n, (dst, kind, src) in enumerate(pieces):
                    done += 1
                    pool.wait_ge(w_rounded, done)
                    one = wv1[:, c, :] if kind == "v" else dst(wqk1)
                    two = wv2[:, c, :] if kind == "v" else dst(wqk2)
                    ins = nc.gpsimd.tensor_tensor(two, src(raw[:, i % 2, :]), one, ALU.subtract)
                ins.then_inc(raw_split, 1)

        def sp_wo(sp, cross):
            name = "o2" if cross else "o1"
            for j in range(GH):
                sp.dma_start(wo[32 * j:32 * j + DH, :, :],
                             w[name + "_w"].rearrange("(g j d) n -> j d g n", j=GH, d=DH)[j]).then_inc(wo_loaded, 16)
            sp.dma_start(wo[DH:DH + 1, 0, :], w[name + "_b"].rearrange("(a n) -> a n", a=1)).then_inc(wo_loaded, 16)

        def products(w1, w2, d1, d2, chunks):
            full = chunks - 1
            return ([(w1(c), d1(c)) for c in range(full)] + [(w2(c), d1(c)) for c in range(full)]
                    + [(w1(full), d1(full)), (w2(full, 64), d1(full, 64))] + [(w1(c), d2(c)) for c in range(full)])

        def tile_products(tile, cross):
            def part(wt, k, chunk=lambda c: c):
                return lambda c, n=P: wt[0:n, chunk(c), k(c) if callable(k) else k, :]
            on_h = (lambda c, n=P: h1[0:n, c, :], lambda c: h2[:, c, :], 3)
            on_c = (lambda c, n=P: c1[0:n, c, :], lambda c: c2[:, :], 2)
            if not cross or tile in (QA, QB):
                return products(part(wqk1, tile), part(wqk2, tile), *on_h)
            if tile in (KA, KB):
                return products(part(wqk1, tile), part(wqk2, tile), *on_c)
            return (products(part(wqk1, QKC), part(wqk2, QKC), *on_h)
                    + products(part(wqk1, lambda c: (KA, KB)[c], lambda c: 2),
                               part(wqk2, lambda c: (KA, KB)[c], lambda c: 2), *on_c))

        def value_products(t, cross):
            toks = slice(t * P, t * P + P)
            d1, d2, n = ((lambda c, n=P: c1[0:n, c, toks], lambda c: c2[:, toks], 2) if cross
                         else (lambda c, n=P: h1[0:n, c, toks], lambda c: h2[:, c, toks], 3))
            got = products(lambda c, n=P: wv1[0:n, c, :], lambda c, n=P: wv2[0:n, c, :], d1, d2, n)
            return [(d, wt) for wt, d in got]

        def dense_plan(cross_next):
            ctx_tiles = [("op", "c0"), ("op", "c1")] if cross_next else []
            plan = {(g, 1): [("mt", g)] for g in range(NG)}
            plan[0, 2] = [("v", 0), ("v", 1)]
            plan[0, 3] = [("v", 2), ("v", 3)]
            plan[1, 0] = [("o", 0), ("o", 1)]
            plan[1, 1] = plan[1, 1] + [("o", 2), ("o", 3)]
            plan[1, 2] = [("op", "t0"), ("op", "t1"), ("op", "t2")]
            plan[1, 3] = ctx_tiles + [("op", QA)]
            plan[2, 0] = [("op", KA)]
            plan[2, 1] = plan[2, 1] + [("op", QKC)]
            plan[2, 2] = [("op", QB)]
            plan[2, 3] = [("op", KB)]
            return plan

        def has(kind, what, g, s_prev, s_next):
            if kind == "op":
                return s_next
            if kind == "o":
                return s_prev
            if kind == "mt":
                return s_next or what + 1 < NG
            return True

        def pe_free_wait(pe, last):
            if last is not None:
                pe.wait_ge(*last)

        def pe_smax(pe, s, g, j, qts):
            h = GH * g + j
            base, hc = 64 * (h % 2), h // 2
            if j == 0 and 0 in qts:
                pe.wait_ge(stacked[(0, 0, 1, 1, 2)[g]], 192 * s + 192)
            for qt in qts:
                pe.wait_ge(smax_free, 80 * s + 4 * h + qt + 1)
                nc.tensor.matmul(ps[:, SM + qt % 2, :], qs[base:base + MAX_ROW, hc, qt * P:qt * P + P],
                                 ks[base:base + MAX_ROW, hc, :], start=True, stop=True).then_inc(smax_ready, 1)

        def pe_st(pe, s, g, j, pair):
            h = GH * g + j
            base, hc = 64 * (h % 2), h // 2
            if j == 0 and pair == 0:
                pe.wait_ge(max_placed, 32 * (NG * s + g) + 32)
            pe.wait_ge(exp_done, 40 * s + 2 * h + pair + 1)
            for kt in (2 * pair, 2 * pair + 1):
                ins = nc.tensor.matmul(ps[:, ST + kt, :], ks[base:base + 64, hc, kt * P:kt * P + P],
                                       qs[base:base + 64, hc, :], start=True, stop=True)
            ins.then_inc(st_ready, 1)

        def pe_pv(pe, s, g, kt):
            if kt == 0:
                pe.wait_ge(norm_done, 2 * (NG * s + g))
                pe.wait_ge(v_evac, NT * s + NT)
            if kt % 2 == 0:
                pe.wait_ge(exp_done, 40 * s + 2 * (GH * g + GH - 1) + kt // 2 + 3)
            for j in range(GH):
                h = GH * g + j
                ins = nc.tensor.matmul(ps[32 * j:32 * j + 32, OB, :], v[:, kt, h, :], pr[:, RING[h], kt, :],
                                       start=(kt == 0), stop=(kt == NT - 1))
            if kt == NT - 1:
                ins.then_inc(o_ready, 1)

        def pe_mt(pe, s, g):
            pe.wait_ge(mh_ready, NG * s + g + 1)
            for qt in range(NT):
                ins = nc.tensor.matmul(ps[0:8, DB, qt * P:qt * P + P],
                                       mh[:, qt, :, :, :].rearrange("p r a h -> p (r a h)"), identb[:, :],
                                       start=True, stop=True)
            ins.then_inc(mt_ready, 1)

        def pe_op(pe, u, cross, what):
            base = ops_base(u, cross)
            if what == "t0":
                pe.wait_ge(xn_ready, NT * 2 * u + NT * 2)
            if what == "c0":
                pe.wait_ge(cn_loaded, 32 * NT * (u - B) + 32 * NT)
            if what in ("t0", "t1", "t2", "c0", "c1"):
                src, c = (xn if what[0] == "t" else cn), int(what[1])
                for t in range(NT):
                    ins = nc.tensor.transpose(ps[:, DB, t * P:t * P + P], src[:, t, c * P:c * P + P], ident[:, :])
            else:
                if what == QA:
                    pe.wait_ge(op_split, base + (5 if cross else 3))
                    pe.wait_ge(raw_split, 9 + 7 * cross)
                todo = tile_products(what, cross)
                for n, (wt, d) in enumerate(todo):
                    ins = nc.tensor.matmul(ps[:, DB, :], wt, d, start=(n == 0), stop=(n == len(todo) - 1))
            ins.then_inc(op_ready, 1)

        def pe_v(pe, cross, t):
            todo = value_products(t, cross)
            for n, (d, wt) in enumerate(todo):
                ins = nc.tensor.matmul(ps[:, DB, 0:D], d, wt, start=(n == 0), stop=(n == len(todo) - 1))
            ins.then_inc(v_ready, 1)

        def pe_oproj(pe, s, cross, t):
            if t == 0:
                pe.wait_ge(norm_done, 2 * NG * s + 2 * NG)
                pe.wait_ge(wo_loaded, 80 * (1 + cross))
            for g in range(NG):
                ins = nc.tensor.matmul(ps[:, DB, 0:D], on[:, g, t * P:t * P + P], wo[:, g, :],
                                       start=(g == 0), stop=(g == NG - 1))
            ins.then_inc(oproj_ready, 1)

        def op_value(u, cross, what):
            return ops_base(u, cross) + ops_of(cross).index(what) + 1

        def pe_slot(pe, s, cross, cross_next, prev, nxt, last):
            plan = dense_plan(cross_next)
            for g in range(NG):
                for j in range(GH):
                    tg, ts = (g + 2, s) if g + 2 < NG else (g + 2 - NG, s + 1)
                    smax = g + 2 < NG or nxt
                    pg, p_s = (g - 1, s) if g else (NG - 1, s - 1)
                    pv = j < 2 and (g > 0 or prev)
                    for half in range(2):
                        if smax:
                            pe_smax(pe, ts, tg, j, (2 * half, 2 * half + 1))
                        pe_st(pe, s, g, j, half)
                        if pv:
                            pe_pv(pe, p_s, pg, 2 * j + half)
                    for kind, what in plan.get((g, j), []):
                        if not has(kind, what, g, prev, nxt):
                            continue
                        pe_free_wait(pe, last)
                        if kind == "mt":
                            mg, ms = (g + 1, s) if g + 1 < NG else (0, s + 1)
                            pe_mt(pe, ms, mg)
                            last = (mt_evac, NG * ms + mg + 1)
                        elif kind == "v":
                            pe_v(pe, cross, what)
                            last = (v_evac, NT * s + what + 1)
                        elif kind == "o":
                            pe_oproj(pe, s - 1, cross_prev(s, cross), what)
                            last = (res_done, NT * (s - 1) + what + 1)
                        else:
                            pe_op(pe, s + 1, cross_next, what)
                            last = (op_evac, op_value(s + 1, cross_next, what))

        def cross_prev(s, cross):
            return cross and not (isinstance(s, int) and s == B)

        def slots(emit):
            emit(0, False, False, False, True)
            yield range(1, B - 1), False
            emit(B - 1, False, True, True, True)
            emit(B, True, True, True, True)
            yield range(B + 1, UNITS - 1), True
            emit(UNITS - 1, True, True, True, False)

        def run_slots(eng, emit):
            for loop, cross in slots(emit):
                with eng.Fori(loop.start, loop.stop) as s:
                    emit(s, cross, cross, True, True)

        block = ctx.enter_context(nc.Block())

        @block.tensor
        def _(pe):
            pe.sem_inc(smax_free, 2)
            pe.sem_inc(exp_done, 2)
            pe.wait_ge(ident_ready, 2)
            pe.wait_ge(const_ready, 5)
            last = None
            for what in OPS_SELF:
                pe_free_wait(pe, last)
                pe_op(pe, 0, False, what)
                last = (op_evac, op_value(0, False, what))
            pe.wait_ge(ones_loaded, 32)
            for g in (0, 1):
                for j in range(GH):
                    pe_smax(pe, 0, g, j, range(NT))
            pe_free_wait(pe, last)
            pe_mt(pe, 0, 0)

            def emit(s, cross, cross_next, prev, nxt):
                pe_slot(pe, s, cross, cross_next, prev, nxt, (mt_evac, NG * s + 1))
            run_slots(pe, emit)
            for kt in range(NT):
                pe_pv(pe, UNITS - 1, NG - 1, kt)
            for t in range(NT):
                if t:
                    pe.wait_ge(res_done, NT * (UNITS - 1) + t)
                pe_oproj(pe, UNITS - 1, True, t)

        def act_exp(act, s, g, j):
            h = GH * g + j
            for pair in range(2):
                act.wait_ge(st_ready, 40 * s + 2 * h + pair + 1)
                nc.scalar.activation(pr[:, RING[h], 2 * pair:2 * pair + 2, :], ps[:, ST + 2 * pair:ST + 2 * pair + 2, :],
                                     ACT.Exp, scale=SCALE).then_inc(exp_done, 1)

        def act_mt(act, s, g):
            act.wait_ge(mt_ready, NG * s + g + 1)
            act.wait_ge(max_placed, 32 * (NG * s + g))
            nc.scalar.activation(mt[:, :], ps[0:8, DB, :], ACT.Copy).then_inc(mt_evac, 1)

        def act_v(act, s, t):
            act.wait_ge(v_ready, NT * s + t + 1)
            nc.scalar.activation(v[:, t, :, 0:DH], ps[:, DB, 0:D].rearrange("p (h d) -> p h d", d=DH),
                                 ACT.Copy).then_inc(v_evac, 1)

        def act_op(act, u, cross, what):
            n = ops_base(u, cross) + ops_of(cross).index(what)
            norm = 1 if cross else 0
            act.wait_ge(op_ready, n + 1)
            k = ops_of(cross).index(what)
            if k >= 2 or not (isinstance(u, int) and u == 0):
                act.wait_ge(op_split, n - 1)
            if what in ("t0", "t1", "t2"):
                c = int(what[1])
                kw = dict(scale=gb[:, norm, c, 0:1], bias=gb[:, norm, c, 1:2])
                one, f = h1[:, c, :], ACT.Identity
            elif what in ("c0", "c1"):
                kw, one, f = {}, c1[:, int(what[1]), :], ACT.Copy
            else:
                kw, one, f = {}, sq[:, what, 0, :], ACT.Copy
                if not (isinstance(u, int) and u == 0):
                    act.wait_ge(stacked[{QA: 0, KA: 0, QB: 1, KB: 1, QKC: 2}[what]], 192 * u)
            nc.scalar.activation(one, ps[:, DB, :], f, **kw)
            nc.scalar.activation(whole[:, k % 2, :], ps[:, DB, :], f, **kw).then_inc(op_evac, 1)

        def act_slot(act, s, cross, cross_next, prev, nxt):
            plan = dense_plan(cross_next)
            for g in range(NG):
                for j in range(GH):
                    act_exp(act, s, g, j)
                    for kind, what in plan.get((g, j), []):
                        if not has(kind, what, g, prev, nxt):
                            continue
                        if kind == "mt":
                            mg, ms = (g + 1, s) if g + 1 < NG else (0, s + 1)
                            act_mt(act, ms, mg)
                        elif kind == "v":
                            act_v(act, s, what)
                        elif kind == "op":
                            act_op(act, s + 1, cross_next, what)
                    if (g, j) == (0, 3) and cross_next and not cross:
                        act_weights(act, True)

        @block.scalar
        def _(act):
            act.wait_ge(small_loaded, 16 * 16)
            act_weights(act, False)
            for what in OPS_SELF:
                act_op(act, 0, False, what)
            act.wait_ge(mt_ready, 1)
            nc.scalar.activation(mt[:, :], ps[0:8, DB, :], ACT.Copy).then_inc(mt_evac, 1)

            def emit(s, cross, cross_next, prev, nxt):
                act_slot(act, s, cross, cross_next, prev, nxt)
            run_slots(act, emit)

        def dve_smax(dve, s, g, j, qt):
            h = GH * g + j
            if j == 0 and qt == 0:
                dve.wait_ge(mh_ready, NG * s + g)
            dve.wait_ge(smax_ready, 80 * s + 4 * h + qt + 1)
            nc.vector.tensor_reduce(nm[:, qt, j % 2, j // 2:j // 2 + 1], ps[:, SM + qt % 2, :], AX_X, ALU.max,
                                    negate=True).then_inc(smax_free, 1)

        def dve_parts(dve, s, g):
            dve.wait_ge(smax_free, 80 * s + 16 * g + 18)
            if not (isinstance(s, int) and s == 0 and g == 0):
                dve.wait_ge(mt_ready, NG * s + g)
            nc.vector.tensor_copy(mh[:, :, :, 0, :], nm[:, :, :, :]).then_inc(norm_step, 1)

        def dve_parts_low(dve, count):
            dve.wait_ge(norm_step, count)
            nc.vector.tensor_tensor(mh[:, :, :, 1, :], nm[:, :, :, :], mh[:, :, :, 0, :],
                                    ALU.subtract).then_inc(mh_ready, 1)

        def dve_stats(dve, u, t):
            if t == 0:
                dve.wait_ge(xl_loaded, 16 * u + 16)
            nc.vector.bn_stats(mv6[:, t, :], xl[:, t, :]).then_inc(stats_raw, 1)

        def dve_stats_end(dve, u):
            if not (isinstance(u, int) and u == 0):
                wait_apart(dve, nmr_ready, u, const_ready)
            wait_apart(dve, stats_raw, NT * u + NT, const_ready)
            for t in range(NT):
                nc.vector.bn_aggr(mv[:, t, :], mv6[:, t, :]).then_inc(stats_mv, 1)
            dve.wait_ge(stats_mv, NT * u + NT)
            nc.vector.tensor_scalar(negmean[:, :], mv[:, :, 0], -1.0, None, ALU.mult).then_inc(stats_ready, 1)
            nc.vector.tensor_scalar(vareps[:, :], mv[:, :, 1], EPS, None, ALU.add).then_inc(stats_ready, 1)

        def dve_res(dve, s, t):
            if t == 0:
                dve.wait_ge(xr_loaded, 16 * s + 16)
            dve.wait_ge(oproj_ready, NT * s + t + 1)
            nc.vector.tensor_tensor(xr[:, t, :], ps[:, DB, 0:D], xr[:, t, :], ALU.add).then_inc(res_done, 1)

        STEPS = 5 + NG * 2 * 3

        def dve_norm(dve, s, g, half, part, step, prev_step):
            cols = slice(half * 256, half * 256 + 256)
            if part == 0:
                if half == 0:
                    wait_apart(dve, o_ready, NG * s + g + 1, const_ready)
                wait_apart(dve, norm_done, 2 * (NG * s + g) + half, const_ready)
                nc.vector.stream_shuffle(rs[:, :], ps[:, OB, cols], [DH] * 32).then_inc(norm_step, 1)
            elif part in (1, 2):
                if part == 1:
                    dve.wait_ge(norm_step, step)
                c = slice((part - 1) * 128, part * 128)
                nc.vector.reciprocal(rs[:, c], rs[:, c]).then_inc(norm_step, 1)
            else:
                dve.wait_ge(norm_step, step)
                nc.vector.tensor_tensor(on[:, g, cols], ps[:, OB, cols], rs[:, :], ALU.mult).then_inc(norm_done, 1)

        def dve_slot(dve, s, cross, cross_next, prev, nxt, before):
            steps = 0
            for g in range(NG):
                for j in range(GH):
                    tg, ts = (g + 2, s) if g + 2 < NG else (g + 2 - NG, s + 1)
                    smax = g + 2 < NG or nxt
                    pg, p_s = (g - 1, s) if g else (NG - 1, s - 1)
                    norm = j >= 2 and (g > 0 or prev)
                    if norm and g == 1 and j == 2 and prev:
                        dve.wait_ge(oproj_ready, NT * s)
                    for qt in range(NT):
                        if smax:
                            dve_smax(dve, ts, tg, j, qt)
                        if norm:
                            dve_norm(dve, p_s, pg, j - 2, qt, before + steps, None)
                            steps += qt < 3
                    if j == 3 and smax:
                        dve_parts(dve, ts, tg)
                        steps += 1
                        dve_parts_low(dve, before + steps)
                    if (g, j) == (0, 2) and nxt:
                        dve_stats(dve, s + 1, 0)
                        dve_stats(dve, s + 1, 1)
                    if (g, j) == (0, 3) and nxt:
                        dve_stats(dve, s + 1, 2)
                        dve_stats(dve, s + 1, 3)
                        dve_stats_end(dve, s + 1)
                    if g == 1 and j < 2 and prev:
                        dve_res(dve, s - 1, 2 * j)
                        dve_res(dve, s - 1, 2 * j + 1)
            return steps

        @block.vector
        def _(dve):
            nc.vector.memset(qs[:, :, :].bitcast(F32), 0.0).then_inc(const_ready, 1)
            nc.vector.memset(ks[:, :, :].bitcast(F32), 0.0).then_inc(const_ready, 1)
            nc.vector.memset(pr[:, 0:3, :, :], 1.0).then_inc(const_ready, 1)
            nc.vector.memset(v[:, :, :, DH:32], 0.0).then_inc(const_ready, 1)
            dve.wait_ge(const_ready, 4)
            nc.vector.memset(v[:, :, :, DH:DH + 1], 1.0).then_inc(const_ready, 1)
            for t in range(NT):
                dve_stats(dve, 0, t)
            dve_stats_end(dve, 0)
            for g in (0, 1):
                for j in range(GH):
                    for qt in range(NT):
                        dve_smax(dve, 0, g, j, qt)
                dve_parts(dve, 0, g)
                dve_parts_low(dve, g + 1)

            def emit(s, cross, cross_next, prev, nxt):
                before = 2 if isinstance(s, int) and s == 0 else STEPS * s + (2 - 6)
                dve_slot(dve, s, cross, cross_next, prev, nxt, before)
            run_slots(dve, emit)
            at = STEPS * UNITS + (2 - 6) - 2
            for half in range(2):
                for part in range(4):
                    dve_norm(dve, UNITS - 1, NG - 1, half, part, at + 3 * half + min(part, 3), None)
            for t in range(NT):
                dve_res(dve, UNITS - 1, t)

        def pool_norm(pool, u, cross):
            pool.wait_ge(stats_ready, 2 * u + 2)
            nc.gpsimd.tensor_tensor(rstd[:, :], vareps[:, :], neghalf[:, :], ALU.pow).then_inc(rstd_ready, 1)
            pool.wait_ge(rstd_ready, u + 1)
            nc.gpsimd.tensor_tensor(nmr[:, :], negmean[:, :], rstd[:, :], ALU.mult).then_inc(nmr_ready, 1)
            wait_apart(pool, nmr_ready, u + 1, ident_ready)
            if not (isinstance(u, int) and u == 0):
                wait_apart(pool, op_ready, ops_base(u - 1, cross and not (isinstance(u, int) and u == B)) + 3, ident_ready)
            for t in range(NT):
                for a, b in ((0, D), (2 * P, D)):
                    to = a if a == 0 else D
                    nc.gpsimd.tensor_scalar(xn[:, t, to:to + b - a], xl[:, t, a:b], rstd[:, t:t + 1], nmr[:, t:t + 1],
                                            ALU.mult, ALU.add).then_inc(xn_ready, 1)

        def pool_split(pool, u, cross, what):
            n = ops_base(u, cross) + ops_of(cross).index(what)
            k = ops_of(cross).index(what)
            pool.wait_ge(op_evac, n + 1)
            if what in ("t2", "c1") or k and ops_of(cross)[k - 1] in ("t2", "c1"):
                pool.wait_ge(op_split, n)
            a = slice(64, P) if what in ("t2", "c1") else slice(0, P)
            one, two = {
                "t0": (h1[:, 0, :], h2[:, 0, :]), "t1": (h1[:, 1, :], h2[:, 1, :]), "t2": (h1[a, 2, :], h1[a, 2, :]),
                "c0": (c1[:, 0, :], c2[:, :]), "c1": (c1[a, 1, :], c1[a, 1, :]),
            }.get(what) or (sq[:, what, 0, :], sq[:, what, 1, :])
            nc.gpsimd.tensor_tensor(two, whole[a, k % 2, :], one, ALU.subtract).then_inc(op_split, 1)

        def pool_slot(pool, s, cross, cross_next, prev, nxt):
            if not nxt:
                return
            pool_norm(pool, s + 1, cross_next)
            if cross_next and not cross:
                pool_weights(pool, True)
            for what in ops_of(cross_next):
                pool_split(pool, s + 1, cross_next, what)

        @block.gpsimd
        def _(pool):
            nc.gpsimd.memset(ident[:, :], 0.0).then_inc(ident_zero, 1)
            nc.gpsimd.memset(identb[:, :], 0.0).then_inc(ident_zero, 1)
            nc.gpsimd.memset(wo[:, :, :], 0.0).then_inc(ident_zero, 1)
            nc.gpsimd.memset(neghalf[:, :], -0.5).then_inc(ident_zero, 1)
            pool.wait_ge(ident_zero, 4)
            for m in (ident, identb):
                nc.gpsimd.affine_select(out=m[:, :], in_=m[:, :], compare_op=ALU.not_equal, fill=1.0, base=0,
                                        pattern=[[-1, P]], channel_multiplier=1).then_inc(ident_ready, 1)
            pool_norm(pool, 0, False)
            pool_weights(pool, False)
            for what in OPS_SELF:
                pool_split(pool, 0, False, what)

            def emit(s, cross, cross_next, prev, nxt):
                pool_slot(pool, s, cross, cross_next, prev, nxt)
            run_slots(pool, emit)

        def tokens(t, b):
            return t[b].rearrange("(t p) d -> p t d", p=P)

        def sp_stack(sp, u, cross, which):
            tiles = {0: (QA, KA), 1: (QB, KB), 2: (QKC, QKC)}[which]
            hc, nh = ((0, 4), (4, 4), (8, 2))[which]
            for side, (stack, tile) in enumerate(zip((qs, ks), tiles)):
                sp.wait_ge(op_split, op_value(u, cross, tile))
                for row, *parts in STACK:
                    for par in range(2):
                        n = 64 if which < 2 else 32
                        first = par * n + (64 * side if which == 2 else 0)
                        sp.dma_start(stack[64 * par + DH * row:64 * par + DH * row + DH, hc:hc + nh, :].bitcast(F32),
                                     sq[first:first + n, tile, parts[side], :].bitcast(F32)).then_inc(stacked[which], 16)

        def sp_max(sp, s, g):
            sp.wait_ge(mt_evac, NG * s + g + 1)
            for par in range(2):
                sp.dma_start(qs[64 * par + MAX_ROW:64 * par + MAX_ROW + 2, 2 * g:2 * g + 2, :].bitcast(F32),
                             mt[4 * par:4 * par + 4, :].bitcast(F32)).then_inc(max_placed, 16)

        def sp_slot(sp, s, cross, cross_next, prev, nxt):
            src = x1 if cross_prev(s, cross) else x
            dst = x2 if cross_prev(s, cross) else x1
            if prev:
                wait_apart(sp, st_ready, 40 * s, ident_zero)
            sp_stack(sp, s, cross, 2)
            if nxt:
                sp.wait_ge(xn_ready, 2 * NT * s + 2 * NT)
                if cross_next:
                    sp.wait_ge(x_stored, 16 * (s - (B - 2)))
                    sp.dma_start(xl[:, :, :], tokens(x1, s - (B - 1))).then_inc(xl_loaded, 16)
                    if cross:
                        sp.wait_ge(op_ready, ops_base(s, True) + 5)
                    for t in range(NT):
                        for a, b in ((0, C), (P, C)):
                            to = a if a == 0 else C
                            sp.dma_start(cn[:, t, to:to + b - a],
                                         ctx_in[s - (B - 1)][t * P:t * P + P, a:b]).then_inc(cn_loaded, 16)
                else:
                    sp.dma_start(xl[:, :, :], tokens(x, s + 1)).then_inc(xl_loaded, 16)
            if prev:
                if not (isinstance(s, int) and s == 1):
                    sp.wait_ge(x_stored, 16 * (s - 1))
                b = s - 1 - (B if cross_prev(s, cross) else 0)
                sp.dma_start(xr[:, :, :], tokens(src, b)).then_inc(xr_loaded, 16)
            sp_max(sp, s, 1)
            if cross_next and not cross:
                sp_weights(sp, True)
            if prev:
                sp.wait_ge(res_done, NT * s)
                sp.dma_start(tokens(dst, b), xr[:, :, :]).then_inc(x_stored, 16)
            if isinstance(s, int) and s == B:
                sp.wait_ge(oproj_ready, NT * B)
                sp_wo(sp, True)
            sp_max(sp, s, 2)
            if nxt:
                wait_apart(sp, st_ready, 40 * s + 16, ident_zero)
                sp_stack(sp, s + 1, cross_next, 0)
            sp_max(sp, s, 3)
            sp_max(sp, s, 4)
            if nxt:
                wait_apart(sp, st_ready, 40 * s + 32, ident_zero)
                sp_stack(sp, s + 1, cross_next, 1)
                sp_max(sp, s + 1, 0)

        @block.sync
        def _(sp):
            sp.dma_start(xl[:, :, :], tokens(x, 0)).then_inc(xl_loaded, 16)
            for k, name in enumerate(("n1", "n2")):
                for q, part in enumerate(("_g", "_b")):
                    vec = w[name + part].rearrange("(p a) -> p a", a=1)
                    sp.dma_start(gb[:, k, 0, q:q + 1], vec[0:P]).then_inc(small_loaded, 16)
                    sp.dma_start(gb[:, k, 1, q:q + 1], vec[P:2 * P]).then_inc(small_loaded, 16)
                    sp.dma_start(gb[0:64, k, 2, q:q + 1], vec[2 * P:D]).then_inc(small_loaded, 16)
                    sp.dma_start(gb[64:P, k, 2, q:q + 1], vec[2 * P:D]).then_inc(small_loaded, 16)
            sp_weights(sp, False)
            sp.wait_ge(ident_zero, 4)
            sp_wo(sp, False)
            sp.wait_ge(const_ready, 5)
            ones = pr[:, 0:3, :, :].rearrange("p a b c -> p (a b c)")[0:2, 0:(H // 2) * N]
            for par in range(2):
                sp.dma_start(ks[64 * par + MAX_ROW:64 * par + MAX_ROW + 2, :, :].bitcast(F32),
                             ones.rearrange("p (h n) -> p h n", n=N)).then_inc(ones_loaded, 16)
            sp_stack(sp, 0, False, 0)
            sp_stack(sp, 0, False, 1)
            sp_max(sp, 0, 0)

            def emit(s, cross, cross_next, prev, nxt):
                sp_slot(sp, s, cross, cross_next, prev, nxt)
            run_slots(sp, emit)
            u = UNITS - 1
            sp.wait_ge(x_stored, 16 * u)
            sp.dma_start(xr[:, :, :], tokens(x1, B - 1)).then_inc(xr_loaded, 16)
            sp.wait_ge(res_done, NT * UNITS)
            sp.dma_start(tokens(x2, B - 1), xr[:, :, :]).then_inc(x_stored, 16)
            sp.wait_ge(x_stored, 16 * UNITS)


def feed_forward(nc, x2, w, out):
    with ExitStack() as ctx:
        def sb(name, shape, dt=F32):
            return ctx.enter_context(nc.sbuf_tensor("ff_" + name, shape, dt))

        def sem(name):
            return ctx.enter_context(nc.semaphore("ff_" + name))

        ps = ctx.enter_context(nc.psum_tensor("ff_ps", [P, 8, 512], F32))
        ACC, AG = 0, 4

        xl = sb("xl", [P, NT, D])
        xr = sb("xr", [P, NT, D])
        y = sb("y", [P, NT, D])
        xn = sb("xn", [P, NT, 3 * P])
        mv6 = sb("mv6", [P, NT, 6])
        mv = sb("mv", [P, NT, 2])
        negmean = sb("negmean", [P, NT])
        vareps = sb("vareps", [P, NT])
        rstd = sb("rstd", [P, NT])
        nmr = sb("nmr", [P, NT])
        neghalf = sb("neghalf", [P, NT])
        gb = sb("gb", [P, 3, 2])
        b1 = sb("b1", [P, 2 * MC])
        b2 = sb("b2", [P, D])
        h1 = sb("h1", [P, 3, N], F32R)
        h2 = sb("h2", [P, 2, N], F32R)
        whole = sb("whole", [P, 3, N])
        gate = sb("gate", [P, 2, N])
        u = sb("u", [P, 3, N])
        u1 = sb("u1", [P, 3, N], F32R)
        u2 = sb("u2", [P, 3, N], F32R)
        raw = sb("raw", [P, 2, 2 * F])
        wa1 = sb("wa1", [P, 3, 2 * F], F32R)
        wa2 = sb("wa2", [P, 3, 2 * F], F32R)
        wb1 = sb("wb1", [P, MC, D], F32R)
        wb2 = sb("wb2", [P, MC, D], F32R)
        ident = sb("ident", [P, P])

        ident_zero = sem("ident_zero")
        ident_ready = sem("ident_ready")
        small_loaded = sem("small_loaded")
        raw_loaded = [sem("raw_loaded0"), sem("raw_loaded1")]
        raw_rounded = sem("raw_rounded")
        raw_split = sem("raw_split")
        xl_loaded = sem("xl_loaded")
        xr_loaded = sem("xr_loaded")
        y_stored = sem("y_stored")
        stats_raw = sem("stats_raw")
        stats_mv = sem("stats_mv")
        stats_ready = sem("stats_ready")
        rstd_ready = sem("rstd_ready")
        nmr_ready = sem("nmr_ready")
        xn_ready = sem("xn_ready")
        t_ready = sem("t_ready")
        t_evac = sem("t_evac")
        t_split = sem("t_split")
        ag_ready = sem("ag_ready")
        gate_ready = sem("gate_ready")
        u_ready = sem("u_ready")
        u1_ready = sem("u1_ready")
        u2_ready = sem("u2_ready")
        acc_ready = sem("acc_ready")
        y_ready = sem("y_ready")
        b2_added = sem("b2_added")

        RAW_FULL = [16, 16, 48, 32, 64]
        HALF = MC // 2

        def raw_tile(i):
            return raw[:, i % 2, :] if i < 3 else raw[:, i % 2, 0:HALF * D].rearrange("p (f n) -> p f n", n=D)

        def parts_of(i):
            if i < 3:
                return wa1[:, i, :], wa2[:, i, :]
            f = slice((i - 3) * HALF, (i - 2) * HALF)
            return wb1[:, f, :], wb2[:, f, :]

        def each_batch(eng, emit):
            emit(0, True)
            with eng.Fori(1, B - 1) as b:
                emit(b, True)
            emit(B - 1, False)

        block = ctx.enter_context(nc.Block())

        def tokens(t, b):
            return t[b].rearrange("(t p) d -> p t d", p=P)

        @block.sync
        def _(sp):
            sp.dma_start(xl[:, :, :], tokens(x2, 0)).then_inc(xl_loaded, 16)
            for q, part in enumerate(("n3_g", "n3_b")):
                vec = w[part].rearrange("(p a) -> p a", a=1)
                sp.dma_start(gb[:, 0, q:q + 1], vec[0:P]).then_inc(small_loaded, 16)
                sp.dma_start(gb[:, 1, q:q + 1], vec[P:2 * P]).then_inc(small_loaded, 16)
                sp.dma_start(gb[0:64, 2, q:q + 1], vec[2 * P:D]).then_inc(small_loaded, 16)
                sp.dma_start(gb[64:P, 2, q:q + 1], vec[2 * P:D]).then_inc(small_loaded, 16)
            for i in range(5):
                if i >= 2:
                    sp.wait_ge(raw_split, i - 1)
                if i < 3:
                    n = chunk_rows(D, i)
                    for at in range(0, P, n):
                        sp.dma_start(raw[at:at + n, i % 2, :], w["ff_w1"][i * P:i * P + n, :])\
                          .then_inc(raw_loaded[i % 2], 16)
                else:
                    sp.dma_start(raw_tile(i), w["ff_w2"].rearrange("(f p) n -> p f n", p=P)
                                 [:, (i - 3) * HALF:(i - 2) * HALF, :]).then_inc(raw_loaded[i % 2], 16)
                if i == 1:
                    sp.dma_start(b1[:, :], w["ff_b1"].rearrange("(c p) -> p c", p=P),
                                 allow_slow_non_contiguous=True).then_inc(small_loaded, 16)
                    sp.dma_start(b2[:, :], w["ff_b2"].rearrange("(a n) -> a n", a=1).broadcast_to([P, D]))\
                      .then_inc(small_loaded, 16)

            def emit(b, nxt):
                if nxt:
                    sp.wait_ge(xn_ready, 2 * NT * b + 2 * NT)
                    sp.dma_start(xl[:, :, :], tokens(x2, b + 1)).then_inc(xl_loaded, 16)
                sp.wait_ge(y_ready, NT * b)
                sp.dma_start(xr[:, :, :], tokens(x2, b)).then_inc(xr_loaded, 16)
                sp.wait_ge(y_ready, NT * b + NT)
                sp.dma_start(tokens(out, b), y[:, :, :]).then_inc(y_stored, 16)
            each_batch(sp, emit)
            sp.wait_ge(y_stored, 16 * B)

        @block.tensor
        def _(pe):
            def transposes(b, waits):
                pe.wait_ge(xn_ready, 2 * NT * b + 2 * NT)
                for c, (bank, free) in enumerate(zip((AG, AG + 1, AG + 2), waits)):
                    if free is not None:
                        pe.wait_ge(u_ready, free)
                    for t in range(NT):
                        ins = nc.tensor.transpose(ps[:, bank, t * P:t * P + P], xn[:, t, c * P:c * P + P], ident[:, :])
                    ins.then_inc(t_ready, 1)

            def pair(b, f):
                if f == 0:
                    pe.wait_ge(t_split, 3 * b + 3)
                elif f == 1:
                    pe.wait_ge(u_ready, MC * b)
                else:
                    pe.wait_ge(u_ready, MC * b + f - 1)
                for side in (1, 0):
                    cols = slice(side * F + f * P, side * F + f * P + P)
                    todo = ([(wa1[:, c, cols], h1[:, c, :]) for c in range(3)]
                            + [(wa2[:, c, cols], h1[:, c, :]) for c in range(2)]
                            + [(wa2[0:64, 2, cols], h1[0:64, 2, :])]
                            + [(wa1[:, c, cols], h2[:, c, :]) for c in range(2)])
                    for n, (wt, d) in enumerate(todo):
                        ins = nc.tensor.matmul(ps[:, AG + 2 * (f % 2) + side, :], wt, d,
                                               start=(n == 0), stop=(n == len(todo) - 1))
                    ins.then_inc(ag_ready, 1)

            def down(b, f):
                if f == 0:
                    pe.wait_ge(y_ready, NT * b)
                pe.wait_ge(u1_ready, MC * b + f + 1)
                for t in range(NT):
                    toks = slice(t * P, t * P + P)
                    nc.tensor.matmul(ps[:, ACC + t, 0:D], u1[:, f % 3, toks], wb1[:, f, :], start=(f == 0), stop=False)
                    ins = nc.tensor.matmul(ps[:, ACC + t, 0:D], u1[:, f % 3, toks], wb2[:, f, :], start=False, stop=False)
                pe.wait_ge(u2_ready, MC * b + f + 1)
                for t in range(NT):
                    toks = slice(t * P, t * P + P)
                    ins = nc.tensor.matmul(ps[:, ACC + t, 0:D], u2[:, f % 3, toks], wb1[:, f, :],
                                           start=False, stop=(f == MC - 1))
                    if f == MC - 1:
                        ins.then_inc(acc_ready, 1)

            pe.wait_ge(ident_ready, 1)
            transposes(0, (None, None, None))
            pe.wait_ge(raw_split, 5)

            def emit(b, nxt):
                for f in range(MC):
                    pair(b, f)
                    if f >= 2:
                        down(b, f - 2)
                if nxt:
                    at = MC * b + MC
                    transposes(b + 1, (at - 1, at - 1, at))
                down(b, MC - 2)
                down(b, MC - 1)
            each_batch(pe, emit)

        @block.scalar
        def _(act):
            def features(b):
                for c in range(3):
                    act.wait_ge(t_ready, 3 * b + c + 1)
                    if c == 0 and not (isinstance(b, int) and b == 0):
                        act.wait_ge(t_split, 3 * b)
                    kw = dict(scale=gb[:, c, 0:1], bias=gb[:, c, 1:2])
                    nc.scalar.activation(h1[:, c, :], ps[:, AG + c, :], ACT.Identity, **kw)
                    nc.scalar.activation(whole[:, c, :], ps[:, AG + c, :], ACT.Identity, **kw).then_inc(t_evac, 1)

            act.wait_ge(small_loaded, 16 * 10)
            for i in range(5):
                act.wait_ge(raw_loaded[i % 2], RAW_FULL[i])
                nc.scalar.activation(parts_of(i)[0], raw_tile(i), ACT.Copy).then_inc(raw_rounded, 1)
                if i == 1:
                    features(0)

            def rounded(b, f):
                act.wait_ge(u_ready, MC * b + f + 1)
                nc.scalar.activation(u1[:, f % 3, :], u[:, f % 3, :], ACT.Copy).then_inc(u1_ready, 1)

            def emit(b, nxt):
                for f in range(MC):
                    act.wait_ge(ag_ready, 2 * MC * b + 2 * f + 1)
                    if f < 2:
                        act.wait_ge(u_ready, MC * b)
                    nc.scalar.activation(gate[:, f % 2, :], ps[:, AG + 2 * (f % 2) + 1, :], ACT.Gelu,
                                         bias=b1[:, MC + f:MC + f + 1]).then_inc(gate_ready, 1)
                    if f:
                        rounded(b, f - 1)
                rounded(b, MC - 1)
                if nxt:
                    features(b + 1)
            each_batch(act, emit)

        @block.vector
        def _(dve):
            def stats(b):
                dve.wait_ge(xl_loaded, 16 * b + 16)
                for t in range(NT):
                    nc.vector.bn_stats(mv6[:, t, :], xl[:, t, :]).then_inc(stats_raw, 1)
                wait_apart(dve, nmr_ready, b, xl_loaded)
                wait_apart(dve, stats_raw, NT * b + NT, xl_loaded)
                for t in range(NT):
                    nc.vector.bn_aggr(mv[:, t, :], mv6[:, t, :]).then_inc(stats_mv, 1)
                dve.wait_ge(stats_mv, NT * b + NT)
                nc.vector.tensor_scalar(negmean[:, :], mv[:, :, 0], -1.0, None, ALU.mult).then_inc(stats_ready, 1)
                nc.vector.tensor_scalar(vareps[:, :], mv[:, :, 1], EPS, None, ALU.add).then_inc(stats_ready, 1)

            stats(0)
            for i in range(5):
                dve.wait_ge(raw_rounded, i + 1)
                one, two = parts_of(i)
                nc.vector.tensor_tensor(two, raw_tile(i), one, ALU.subtract).then_inc(raw_split, 1)

            def emit(b, nxt):
                for f in range(MC):
                    dve.wait_ge(ag_ready, 2 * MC * b + 2 * f + 2)
                    dve.wait_ge(gate_ready, MC * b + f + 1)
                    if f < 3:
                        dve.wait_ge(u2_ready, MC * b)
                    else:
                        dve.wait_ge(u2_ready, MC * b + f - 2)
                    nc.vector.scalar_tensor_tensor(out=u[:, f % 3, :], in0=ps[:, AG + 2 * (f % 2), :],
                                                   scalar=b1[:, f:f + 1], in1=gate[:, f % 2, :],
                                                   op0=ALU.add, op1=ALU.mult).then_inc(u_ready, 1)
                    if f == 1 and nxt:
                        stats(b + 1)
                dve.wait_ge(b2_added, NT * b + NT)
                dve.wait_ge(y_stored, 16 * b)
                for t in range(NT):
                    dve.wait_ge(acc_ready, NT * b + t + 1)
                    nc.vector.tensor_tensor(y[:, t, :], ps[:, ACC + t, 0:D], xr[:, t, :], ALU.add).then_inc(y_ready, 1)
            each_batch(dve, emit)

        @block.gpsimd
        def _(pool):
            nc.gpsimd.memset(ident[:, :], 0.0).then_inc(ident_zero, 1)
            nc.gpsimd.memset(neghalf[:, :], -0.5).then_inc(ident_zero, 1)
            pool.wait_ge(ident_zero, 2)
            nc.gpsimd.affine_select(out=ident[:, :], in_=ident[:, :], compare_op=ALU.not_equal, fill=1.0, base=0,
                                    pattern=[[-1, P]], channel_multiplier=1).then_inc(ident_ready, 1)

            def norm(b):
                pool.wait_ge(stats_ready, 2 * b + 2)
                nc.gpsimd.tensor_tensor(rstd[:, :], vareps[:, :], neghalf[:, :], ALU.pow).then_inc(rstd_ready, 1)
                pool.wait_ge(rstd_ready, b + 1)
                nc.gpsimd.tensor_tensor(nmr[:, :], negmean[:, :], rstd[:, :], ALU.mult).then_inc(nmr_ready, 1)
                wait_apart(pool, nmr_ready, b + 1, ident_ready)
                wait_apart(pool, t_ready, 3 * b, ident_ready)
                for t in range(NT):
                    for a, e in ((0, D), (2 * P, D)):
                        to = a if a == 0 else D
                        nc.gpsimd.tensor_scalar(xn[:, t, to:to + e - a], xl[:, t, a:e], rstd[:, t:t + 1],
                                                nmr[:, t:t + 1], ALU.mult, ALU.add).then_inc(xn_ready, 1)

            def features(b):
                for c in range(3):
                    pool.wait_ge(t_evac, 3 * b + c + 1)
                    if c == 2:
                        pool.wait_ge(t_split, 3 * b + 2)
                    a = slice(64, P) if c == 2 else slice(0, P)
                    two = h1[a, 2, :] if c == 2 else h2[:, c, :]
                    nc.gpsimd.tensor_tensor(two, whole[a, c, :], h1[a, c, :], ALU.subtract).then_inc(t_split, 1)
                pool.wait_ge(t_split, 3 * b + 3)

            norm(0)
            features(0)
            pool.wait_ge(small_loaded, 16 * 10)

            def emit(b, nxt):
                for f in range(MC):
                    pool.wait_ge(u1_ready, MC * b + f + 1)
                    nc.gpsimd.tensor_tensor(u2[:, f % 3, :], u[:, f % 3, :], u1[:, f % 3, :],
                                            ALU.subtract).then_inc(u2_ready, 1)
                    if f == 2 and nxt:
                        norm(b + 1)
                    if f == 4:
                        pool.wait_ge(xr_loaded, 16 * b + 16)
                        for t in range(NT):
                            nc.gpsimd.tensor_tensor(xr[:, t, :], xr[:, t, :], b2[:, :], ALU.add).then_inc(b2_added, 1)
                if nxt:
                    features(b + 1)
            each_batch(pool, emit)


def layer(nc, x, ctx_in, w, out):
    x1 = nc.dram_tensor("x_after_self", [B, N, D], F32).ap()
    x2 = nc.dram_tensor("x_after_cross", [B, N, D], F32).ap()
    attention(nc, x, ctx_in, w, x1, x2)
    feed_forward(nc, x2, w, out)


_WEIGHTS = ["n1_g", "n1_b", "q1", "k1", "v1", "o1_w", "o1_b", "n2_g", "n2_b", "q2", "k2", "v2", "o2_w", "o2_b",
            "n3_g", "n3_b", "ff_w1", "ff_b1", "ff_w2", "ff_b2"]


def kernel(**inputs):
    import numpy as _np
    import concourse.bacc as _bacc
    from concourse import mybir as _mybir
    from concourse.bass_utils import run_bass_kernel_spmd as _run

    nc = _bacc.Bacc("TRN2", target_bir_lowering=False, num_devices=1)
    arrays, aps = {}, {}
    for name in ["x", "ctx_768"] + ["L0_xattn_" + n for n in _WEIGHTS]:
        a = _np.ascontiguousarray(inputs[name])
        arrays[f"in_{name}_dram"] = a
        aps[name] = nc.dram_tensor(f"in_{name}_dram", a.shape, _mybir.dt.from_np(a.dtype), kind="ExternalInput").ap()
    out = nc.dram_tensor("out_0_dram", (B, N, D), _mybir.dt.float32, kind="ExternalOutput").ap()
    layer(nc, aps["x"], aps["ctx_768"], {n: aps["L0_xattn_" + n] for n in _WEIGHTS}, out)
    r = _run(nc, [arrays], core_ids=[0])
    return r.results[0]["out_0_dram"]
```

```python
from contextlib import ExitStack

import concourse.bass as bass
from concourse import mybir

F32 = mybir.dt.float32
F32R = mybir.dt.float32r
BF16 = mybir.dt.bfloat16
ALU = mybir.AluOpType
ACT = mybir.ActivationFunctionType
AX_X = mybir.AxisListType.X

P = 128
B, N, D, C = 8, 512, 320, 192
H, DH = 20, 16
F = 1280
EPS = 1e-5
SCALE = DH ** -0.5
NT = N // P
GH = 4
NG = H // GH
UNITS = 2 * B
MAX_ROW = 96
MC = F // P

QA, KA, QKC, QB, KB = range(5)
STACK = [(0, 0, 0), (1, 1, 0), (2, 0, 1)]
STACK_DMAS = 16 * 3 * (1 + 2)
STAGE = [0, 1, 2, 0, 1]
RING = [0, 1, 2, 3, 4, 5, 0, 1, 2, 3, 4, 5, 0, 1, 2, 3, 4, 5, 2, 3]

OPS_SELF = ["t0", "t1", "t2", QA, KA, QKC, QB, KB]
OPS_CROSS = ["t0", "t1", "t2", QA, "c0", "c1", KA, QKC, QB, KB]


def ops_of(cross):
    return OPS_CROSS if cross else OPS_SELF


def ops_base(u, cross):
    return 10 * u - 2 * B if cross else 8 * u


def chunk_rows(width, c):
    return min(P, width - c * P)


def wait_apart(eng, sem, value, passed):
    if not isinstance(value, int):
        eng.lower_val(value)
    eng.wait_ge(passed, 1)
    eng.wait_ge(sem, value)


def attention(nc, x, ctx_in, w, x1, x2):
    with ExitStack() as ctx:
        def sb(name, shape, dt=F32):
            return ctx.enter_context(nc.sbuf_tensor(name, shape, dt))

        def sem(name):
            return ctx.enter_context(nc.semaphore(name))

        ps = ctx.enter_context(nc.psum_tensor("ps", [P, 8, 512], F32))
        ST, SM, OB, DB = 0, 4, 6, 7

        xn = sb("xn", [P, NT, 3 * P])
        xr = sb("xr", [P, NT, D])
        cn = sb("cn", [P, NT, 2 * P])
        mv6 = sb("mv6", [P, NT, 6])
        mv = sb("mv", [P, NT, 2])
        negmean = sb("negmean", [P, NT])
        vareps = sb("vareps", [P, NT])
        rstd = sb("rstd", [P, NT])
        nmr = sb("nmr", [P, NT])
        neghalf = sb("neghalf", [P, NT])
        gb = sb("gb", [P, 2, 3, 2])
        h1 = sb("h1", [P, 3, N], F32R)
        h2 = sb("h2", [P, 2, N], F32R)
        c1 = sb("c1", [P, 2, N], F32R)
        c2 = sb("c2", [P, N], F32R)
        whole = sb("whole", [P, 2, N])
        raw = sb("raw", [P, 2, D])
        wqk1 = sb("wqk1", [P, 3, 5, P], F32R)
        wqk2 = sb("wqk2", [P, 3, 5, P], F32R)
        wv1 = sb("wv1", [P, 3, D], F32R)
        wv2 = sb("wv2", [P, 3, D], F32R)
        wo = sb("wo", [P, NG, D])
        sq = sb("sq", [P, 3, 2, N], F32R)
        qs = sb("qs", [P, H // 2, N], F32R)
        ks = sb("ks", [P, H, N], F32R)
        v = sb("v", [P, NT, H, DH + 1])
        pr = sb("pr", [P, 6, NT, N])
        on = sb("on", [P, NG, N])
        sums = sb("sums", [P, GH * N // P])
        inv = sb("inv", [P, GH * N // P])
        rs = sb("rs", [P, N])
        nm = sb("nm", [P, NT, 2, 2])
        mh = sb("mh", [P, NT, 2, 2, 2], BF16)
        mt = sb("mt", [8, N], F32R)
        ident = sb("ident", [P, P])
        identb = sb("identb", [P, P], BF16)

        const_ready = sem("const_ready")
        ident_zero = sem("ident_zero")
        ident_ready = sem("ident_ready")
        ones_loaded = sem("ones_loaded")
        small_loaded = sem("small_loaded")
        wo_loaded = sem("wo_loaded")
        raw_loaded = [sem("raw_loaded0"), sem("raw_loaded1")]
        raw_split = sem("raw_split")
        w_rounded = sem("w_rounded")
        w_zeroed = sem("w_zeroed")
        xl_loaded = sem("xl_loaded")
        cn_loaded = sem("cn_loaded")
        xr_loaded = sem("xr_loaded")
        x_stored = sem("x_stored")
        stats_raw = sem("stats_raw")
        stats_mv = sem("stats_mv")
        stats_ready = sem("stats_ready")
        rstd_ready = sem("rstd_ready")
        nmr_ready = sem("nmr_ready")
        xn_ready = sem("xn_ready")
        op_ready = sem("op_ready")
        op_evac = sem("op_evac")
        op_split = sem("op_split")
        v_ready = sem("v_ready")
        v_evac = sem("v_evac")
        stacked = [sem("stacked_a"), sem("stacked_b"), sem("stacked_c")]
        smax_ready = sem("smax_ready")
        smax_free = sem("smax_free")
        mh_ready = sem("mh_ready")
        mt_ready = sem("mt_ready")
        mt_evac = sem("mt_evac")
        max_placed = sem("max_placed")
        st_ready = sem("st_ready")
        exp_done = sem("exp_done")
        o_ready = sem("o_ready")
        o_evac = sem("o_evac")
        sums_spread = sem("sums_spread")
        inv_ready = sem("inv_ready")
        inv_placed = sem("inv_placed")
        rs_ready = sem("rs_ready")
        mh_high = sem("mh_high")
        norm_done = sem("norm_done")
        oproj_ready = sem("oproj_ready")
        res_done = sem("res_done")

        def weight_chunks(cross):
            pre = "2" if cross else "1"
            wide = C if cross else D
            return ([("q" + pre, D, c) for c in range(3)] + [("k" + pre, wide, c) for c in range((wide + P - 1) // P)]
                    + [("v" + pre, wide, c) for c in range((wide + P - 1) // P)])

        def weight_pieces(name, c):
            src = raw[:, 0, :]
            out = []
            if name[0] == "v":
                return [(lambda t: t[0][:, c, :], "v", lambda r: r)]
            first = {"q": 0, "k": 1}[name[0]]
            for tile, h0, nh in ((QA + first, 0, 8), (QB + first, 8, 8), (QKC, 16, 4)):
                def dst(wt, tile=tile, nh=nh):
                    if name == "k2" and nh == 4:
                        a = wt[:, 2, (KA, KB)[c], 64:128]
                    elif nh == 4:
                        a = wt[:, c, tile, 64 * first:64 * first + 64]
                    else:
                        a = wt[:, c, tile, :]
                    return a.rearrange("p (r d h) -> p r d h", r=2, d=DH)

                def src_of(r, h0=h0, nh=nh):
                    return r[:, DH * h0:DH * (h0 + nh)].rearrange("p (h r d) -> p r d h", r=2, d=DH)
                out.append((dst, "qk", src_of))
            return out

        chunks_before = {False: 0, True: len(weight_chunks(False))}
        pieces_before = {False: 0, True: sum(len(weight_pieces(n, c)) for n, _, c in weight_chunks(False))}

        def sp_weights(sp, cross):
            for i, (name, wide, c) in enumerate(weight_chunks(cross), chunks_before[cross]):
                if i >= 2:
                    sp.wait_ge(raw_split, i - 1)
                n = chunk_rows(wide, c)
                for at in range(0, P, n):
                    sp.dma_start(raw[at:at + n, i % 2, :], w[name][c * P:c * P + n, :]).then_inc(raw_loaded[i % 2], 16)

        def raw_full(i):
            plan = weight_chunks(False) + weight_chunks(True)
            return sum(16 * (P // chunk_rows(wide, c)) for _, wide, c in plan[i % 2:i + 1:2])

        def act_weights(act, cross):
            if cross:
                act.wait_ge(v_ready, NT * B)
                act.wait_ge(w_zeroed, 4)
            for i, (name, wide, c) in enumerate(weight_chunks(cross), chunks_before[cross]):
                act.wait_ge(raw_loaded[i % 2], raw_full(i))
                for dst, kind, src in weight_pieces(name, c):
                    to = wv1[:, c, :] if kind == "v" else dst(wqk1)
                    nc.scalar.activation(to, src(raw[:, i % 2, :]), ACT.Copy).then_inc(w_rounded, 1)

        def pool_weights(pool, cross):
            done = pieces_before[cross]
            if cross:
                pool.wait_ge(v_ready, NT * B)
                for wt in (wqk1, wqk2):
                    nc.gpsimd.memset(wt[:, :, QKC, 64:128].bitcast(F32), 0.0).then_inc(w_zeroed, 1)
                    nc.gpsimd.memset(wt[:, 2, 1:5:3, 0:64].bitcast(F32), 0.0).then_inc(w_zeroed, 1)
                pool.wait_ge(w_zeroed, 4)
            for i, (name, wide, c) in enumerate(weight_chunks(cross), chunks_before[cross]):
                pieces = weight_pieces(name, c)
                for n, (dst, kind, src) in enumerate(pieces):
                    done += 1
                    pool.wait_ge(w_rounded, done)
                    one = wv1[:, c, :] if kind == "v" else dst(wqk1)
                    two = wv2[:, c, :] if kind == "v" else dst(wqk2)
                    ins = nc.gpsimd.tensor_tensor(two, src(raw[:, i % 2, :]), one, ALU.subtract)
                ins.then_inc(raw_split, 1)

        def sp_wo(sp, cross):
            name = "o2" if cross else "o1"
            for j in range(GH):
                sp.dma_start(wo[32 * j:32 * j + DH, :, :],
                             w[name + "_w"].rearrange("(g j d) n -> j d g n", j=GH, d=DH)[j]).then_inc(wo_loaded, 16)
            sp.dma_start(wo[DH:DH + 1, 0, :], w[name + "_b"].rearrange("(a n) -> a n", a=1)).then_inc(wo_loaded, 16)

        def products(w1, w2, d1, d2, chunks):
            full = chunks - 1
            return ([(w1(c), d1(c)) for c in range(full)] + [(w2(c), d1(c)) for c in range(full)]
                    + [(w1(full), d1(full)), (w2(full, 64), d1(full, 64))] + [(w1(c), d2(c)) for c in range(full)])

        def tile_products(tile, cross):
            def part(wt, k, chunk=lambda c: c):
                return lambda c, n=P: wt[0:n, chunk(c), k(c) if callable(k) else k, :]
            on_h = (lambda c, n=P: h1[0:n, c, :], lambda c: h2[:, c, :], 3)
            on_c = (lambda c, n=P: c1[0:n, c, :], lambda c: c2[:, :], 2)
            if not cross or tile in (QA, QB):
                return products(part(wqk1, tile), part(wqk2, tile), *on_h)
            if tile in (KA, KB):
                return products(part(wqk1, tile), part(wqk2, tile), *on_c)
            return (products(part(wqk1, QKC), part(wqk2, QKC), *on_h)
                    + products(part(wqk1, lambda c: (KA, KB)[c], lambda c: 2),
                               part(wqk2, lambda c: (KA, KB)[c], lambda c: 2), *on_c))

        def value_products(t, cross):
            toks = slice(t * P, t * P + P)
            d1, d2, n = ((lambda c, n=P: c1[0:n, c, toks], lambda c: c2[:, toks], 2) if cross
                         else (lambda c, n=P: h1[0:n, c, toks], lambda c: h2[:, c, toks], 3))
            got = products(lambda c, n=P: wv1[0:n, c, :], lambda c, n=P: wv2[0:n, c, :], d1, d2, n)
            return [(d, wt) for wt, d in got]

        def dense_plan(cross_next):
            plan = {2: ("mt", 0), 11: ("mt", 1), 20: ("mt", 2), 26: ("mt", 3), 34: ("mt", 4)}
            plan.update({4 + t: ("v", t) for t in range(NT)})
            plan.update({8 + c: ("op", f"t{c}") for c in range(3)})
            plan.update({12 + t: ("o", t) for t in range(NT)})
            plan.update({16: ("op", QA), 21: ("op", QKC), 25: ("op", QB), 28: ("op", KB)})
            plan.update({17: ("op", "c0"), 18: ("op", "c1"), 19: ("op", KA)} if cross_next else {18: ("op", KA)})
            return plan

        EVAC = [15, 12, 12, 12, 12]
        INV = [17, 15, 14, 14, 14]
        SPREAD = [19, 17, 16, 16, 16]

        def due(after, at, s, prev):
            for g in range(NG):
                if 8 * g + after[g] == at:
                    return s, g
                if 8 * g + after[g] == at + 8 * NG and prev:
                    return s - 1, g
            return None

        def has(kind, what, g, s_prev, s_next):
            if kind == "op":
                return s_next
            if kind == "o":
                return s_prev
            if kind == "mt":
                return s_next or what + 1 < NG
            return True

        def pe_free_wait(pe, last):
            if last is not None:
                pe.wait_ge(*last)

        def pe_smax(pe, s, g, j, qts):
            h = GH * g + j
            if j == 0 and 0 in qts:
                pe.wait_ge(stacked[(0, 0, 1, 1, 2)[g]], STACK_DMAS * (s + 1))
            for qt in qts:
                pe.wait_ge(smax_free, 80 * s + 4 * h + qt + 1)
                nc.tensor.matmul(ps[:, SM + qt % 2, :], qs[0:MAX_ROW, h // 2, qt * P:qt * P + P],
                                 ks[0:MAX_ROW, h, :], start=True, stop=True).then_inc(smax_ready, 1)

        def pe_st(pe, s, g, j, pair):
            h = GH * g + j
            if j == 0 and pair == 0:
                pe.wait_ge(max_placed, 16 * (NG * s + g) + 16)
            pe.wait_ge(exp_done, 40 * s + 2 * h + pair + 1)
            for kt in (2 * pair, 2 * pair + 1):
                ins = nc.tensor.matmul(ps[:, ST + kt, :], ks[:, h, kt * P:kt * P + P],
                                       qs[:, h // 2, :], start=True, stop=True)
            ins.then_inc(st_ready, 1)

        def pe_pv(pe, s, g, kt):
            if kt == 0:
                if not (isinstance(s, int) and s == 0 and g == 0):
                    pe.wait_ge(o_evac, NG * s + g)
                pe.wait_ge(v_evac, NT * s + NT)
            if kt % 2 == 0:
                pe.wait_ge(exp_done, 40 * s + 2 * (GH * g + GH - 1) + kt // 2 + 3)
            for j in range(GH):
                h = GH * g + j
                ins = nc.tensor.matmul(ps[32 * j:32 * j + DH + 1, OB, :], v[:, kt, h, :], pr[:, RING[h], kt, :],
                                       start=(kt == 0), stop=(kt == NT - 1))
            if kt == NT - 1:
                ins.then_inc(o_ready, 1)

        def pe_mt(pe, s, g):
            pe.wait_ge(mh_ready, NG * s + g + 1)
            for qt in range(NT):
                ins = nc.tensor.matmul(ps[0:8, DB, qt * P:qt * P + P],
                                       mh[:, qt, :, :, :].rearrange("p r a h -> p (r a h)"), identb[:, :],
                                       start=True, stop=True)
            ins.then_inc(mt_ready, 1)

        def pe_op(pe, u, cross, what):
            base = ops_base(u, cross)
            if what == "t0":
                pe.wait_ge(xn_ready, NT * u + NT)
            if what == "c0":
                pe.wait_ge(cn_loaded, 32 * (u - B) + 32)
            if what in ("t0", "t1", "t2", "c0", "c1"):
                src, c = (xn if what[0] == "t" else cn), int(what[1])
                for t in range(NT):
                    ins = nc.tensor.transpose(ps[:, DB, t * P:t * P + P], src[:, t, c * P:c * P + P], ident[:, :])
            else:
                if what == QA:
                    pe.wait_ge(op_split, base + 3)
                    pe.wait_ge(raw_split, 9 + 7 * cross)
                if what == KA and cross:
                    pe.wait_ge(op_split, op_value(u, cross, "c1"))
                todo = tile_products(what, cross)
                for n, (wt, d) in enumerate(todo):
                    ins = nc.tensor.matmul(ps[:, DB, :], wt, d, start=(n == 0), stop=(n == len(todo) - 1))
            ins.then_inc(op_ready, 1)

        def pe_v(pe, cross, t):
            todo = value_products(t, cross)
            for n, (d, wt) in enumerate(todo):
                ins = nc.tensor.matmul(ps[:, DB, 0:D], d, wt, start=(n == 0), stop=(n == len(todo) - 1))
            ins.then_inc(v_ready, 1)

        def pe_oproj(pe, s, cross, t):
            if t == 0:
                pe.wait_ge(norm_done, NG * s + NG)
                pe.wait_ge(wo_loaded, 80 * (1 + cross))
            for g in range(NG):
                ins = nc.tensor.matmul(ps[:, DB, 0:D], on[:, g, t * P:t * P + P], wo[:, g, :],
                                       start=(g == 0), stop=(g == NG - 1))
            ins.then_inc(oproj_ready, 1)

        def op_value(u, cross, what):
            return ops_base(u, cross) + ops_of(cross).index(what) + 1

        def pe_slot(pe, s, cross, cross_next, prev, nxt, last):
            plan = dense_plan(cross_next)
            for g in range(NG):
                for j in range(GH):
                    tg, ts = (g + 2, s) if g + 2 < NG else (g + 2 - NG, s + 1)
                    smax = g + 2 < NG or nxt
                    pg, p_s = (g - 1, s) if g else (NG - 1, s - 1)
                    pv = j < 2 and (g > 0 or prev)
                    for half in range(2):
                        if smax:
                            pe_smax(pe, ts, tg, j, (2 * half, 2 * half + 1))
                        pe_st(pe, s, g, j, half)
                        if pv:
                            pe_pv(pe, p_s, pg, 2 * j + half)
                        kind, what = plan.get(8 * g + 2 * j + half, (None, None))
                        if kind is None or not has(kind, what, g, prev, nxt):
                            continue
                        pe_free_wait(pe, last)
                        if kind == "mt":
                            mg, ms = (g + 1, s) if g + 1 < NG else (0, s + 1)
                            pe_mt(pe, ms, mg)
                            last = (mt_evac, NG * ms + mg + 1)
                        elif kind == "v":
                            pe_v(pe, cross, what)
                            last = (v_evac, NT * s + what + 1)
                        elif kind == "o":
                            pe_oproj(pe, s - 1, cross_prev(s, cross), what)
                            last = (res_done, NT * (s - 1) + what + 1)
                        else:
                            pe_op(pe, s + 1, cross_next, what)
                            last = (op_evac, op_value(s + 1, cross_next, what))

        def cross_prev(s, cross):
            return cross and not (isinstance(s, int) and s == B)

        def slots(emit):
            emit(0, False, False, False, True)
            yield range(1, B - 1), False
            emit(B - 1, False, True, True, True)
            emit(B, True, True, True, True)
            yield range(B + 1, UNITS - 1), True
            emit(UNITS - 1, True, True, True, False)

        def run_slots(eng, emit):
            for loop, cross in slots(emit):
                with eng.Fori(loop.start, loop.stop) as s:
                    emit(s, cross, cross, True, True)

        block = ctx.enter_context(nc.Block())

        @block.tensor
        def _(pe):
            pe.sem_inc(smax_free, 2)
            pe.sem_inc(exp_done, 2)
            pe.wait_ge(ident_ready, 2)
            last = None
            for what in OPS_SELF:
                pe_free_wait(pe, last)
                pe_op(pe, 0, False, what)
                last = (op_evac, op_value(0, False, what))
            pe.wait_ge(ones_loaded, 32)
            pe.wait_ge(const_ready, 6)
            for g in (0, 1):
                for j in range(GH):
                    pe_smax(pe, 0, g, j, range(NT))
            pe_free_wait(pe, last)
            pe_mt(pe, 0, 0)

            def emit(s, cross, cross_next, prev, nxt):
                pe_slot(pe, s, cross, cross_next, prev, nxt, (mt_evac, NG * s + 1))
            run_slots(pe, emit)
            for kt in range(NT):
                pe_pv(pe, UNITS - 1, NG - 1, kt)
            for t in range(NT):
                if t:
                    pe.wait_ge(res_done, NT * (UNITS - 1) + t)
                pe_oproj(pe, UNITS - 1, True, t)

        def act_exp(act, s, g, j, pair):
            h = GH * g + j
            act.wait_ge(st_ready, 40 * s + 2 * h + pair + 1)
            nc.scalar.activation(pr[:, RING[h], 2 * pair:2 * pair + 2, :], ps[:, ST + 2 * pair:ST + 2 * pair + 2, :],
                                 ACT.Exp, scale=SCALE).then_inc(exp_done, 1)

        def act_mt(act, s, g):
            act.wait_ge(mt_ready, NG * s + g + 1)
            act.wait_ge(max_placed, 16 * (NG * s + g))
            nc.scalar.activation(mt[:, :], ps[0:8, DB, :], ACT.Copy).then_inc(mt_evac, 1)

        def act_o(act, s, g):
            act.wait_ge(o_ready, NG * s + g + 1)
            if g == 0 and not (isinstance(s, int) and s == 0):
                act.wait_ge(oproj_ready, NT * s)
            nc.scalar.activation(on[:, g, :], ps[:, OB, :], ACT.Copy).then_inc(o_evac, 1)

        def act_v(act, s, t):
            act.wait_ge(v_ready, NT * s + t + 1)
            nc.scalar.activation(v[:, t, :, 0:DH], ps[:, DB, 0:D].rearrange("p (h d) -> p h d", d=DH),
                                 ACT.Copy).then_inc(v_evac, 1)

        def act_op(act, u, cross, what):
            n = ops_base(u, cross) + ops_of(cross).index(what)
            norm = 1 if cross else 0
            act.wait_ge(op_ready, n + 1)
            k = ops_of(cross).index(what)
            if k >= 2 or not (isinstance(u, int) and u == 0):
                act.wait_ge(op_split, n - 1)
            if what in ("t0", "t1", "t2"):
                c = int(what[1])
                kw = dict(scale=gb[:, norm, c, 0:1], bias=gb[:, norm, c, 1:2])
                one, f = h1[:, c, :], ACT.Identity
            elif what in ("c0", "c1"):
                kw, one, f = {}, c1[:, int(what[1]), :], ACT.Copy
            else:
                kw, one, f = {}, sq[:, STAGE[what], 0, :], ACT.Copy
                before, sets = {QA: (1, u), KA: (1, u), QKC: (2, u), QB: (0, u + 1), KB: (0, u + 1)}[what]
                if not (isinstance(sets, int) and sets == 0):
                    act.wait_ge(stacked[before], STACK_DMAS * sets)
            nc.scalar.activation(one, ps[:, DB, :], f, **kw)
            nc.scalar.activation(whole[:, k % 2, :], ps[:, DB, :], f, **kw).then_inc(op_evac, 1)

        def act_slot(act, s, cross, cross_next, prev, nxt):
            plan = dense_plan(cross_next)
            for at in range(8 * NG):
                g, j, half = at // 8, at // 2 % GH, at % 2
                act_exp(act, s, g, j, half)
                kind, what = plan.get(at, (None, None))
                if kind is not None and has(kind, what, g, prev, nxt):
                    if kind == "mt":
                        mg, ms = (g + 1, s) if g + 1 < NG else (0, s + 1)
                        act_mt(act, ms, mg)
                    elif kind == "v":
                        act_v(act, s, what)
                    elif kind == "op":
                        act_op(act, s + 1, cross_next, what)
                group = due(EVAC, at, s, prev)
                if group:
                    act_o(act, *group)
                if at == 7 and cross_next and not cross:
                    act_weights(act, True)

        @block.scalar
        def _(act):
            act.wait_ge(small_loaded, 16 * 16)
            act_weights(act, False)
            for what in OPS_SELF:
                act_op(act, 0, False, what)
            act.wait_ge(mt_ready, 1)
            nc.scalar.activation(mt[:, :], ps[0:8, DB, :], ACT.Copy).then_inc(mt_evac, 1)

            def emit(s, cross, cross_next, prev, nxt):
                act_slot(act, s, cross, cross_next, prev, nxt)
            run_slots(act, emit)
            act_o(act, UNITS - 1, NG - 1)

        def dve_smax(dve, s, g, j, qt):
            h = GH * g + j
            if j == 0 and qt == 0:
                dve.wait_ge(mh_ready, NG * s + g)
            dve.wait_ge(smax_ready, 80 * s + 4 * h + qt + 1)
            nc.vector.tensor_reduce(nm[:, qt, j % 2, j // 2:j // 2 + 1], ps[:, SM + qt % 2, :], AX_X, ALU.max,
                                    negate=True).then_inc(smax_free, 1)

        def dve_parts(dve, s, g):
            dve.wait_ge(smax_free, 80 * s + 16 * g + 18)
            if not (isinstance(s, int) and s == 0 and g == 0):
                dve.wait_ge(mt_ready, NG * s + g)
            nc.vector.tensor_copy(mh[:, :, :, 0, :], nm[:, :, :, :]).then_inc(mh_high, 1)
            dve.wait_ge(mh_high, NG * s + g + 1)
            nc.vector.tensor_tensor(mh[:, :, :, 1, :], nm[:, :, :, :], mh[:, :, :, 0, :],
                                    ALU.subtract).then_inc(mh_ready, 1)

        def dve_stats(dve, u, t):
            if t == 0:
                dve.wait_ge(xl_loaded, 32 * u + 32)
            nc.vector.bn_stats(mv6[:, t, :], xn[:, t, 0:D]).then_inc(stats_raw, 1)

        def dve_stats_end(dve, u):
            if not (isinstance(u, int) and u == 0):
                wait_apart(dve, nmr_ready, u, const_ready)
            wait_apart(dve, stats_raw, NT * u + NT, const_ready)
            for t in range(NT):
                nc.vector.bn_aggr(mv[:, t, :], mv6[:, t, :]).then_inc(stats_mv, 1)
            dve.wait_ge(stats_mv, NT * u + NT)
            nc.vector.tensor_scalar(negmean[:, :], mv[:, :, 0], -1.0, None, ALU.mult).then_inc(stats_ready, 1)
            nc.vector.tensor_scalar(vareps[:, :], mv[:, :, 1], EPS, None, ALU.add).then_inc(stats_ready, 1)

        def dve_res(dve, s, t):
            if t == 0:
                dve.wait_ge(xr_loaded, 16 * s + 16)
            dve.wait_ge(oproj_ready, NT * s + t + 1)
            nc.vector.tensor_tensor(xr[:, t, :], ps[:, DB, 0:D], xr[:, t, :], ALU.add).then_inc(res_done, 1)

        def dve_inv(dve, s, g):
            dve.wait_ge(sums_spread, 16 * (NG * s + g) + 16)
            if not (isinstance(s, int) and s == 0 and g == 0):
                dve.wait_ge(inv_placed, 16 * (NG * s + g))
            nc.vector.reciprocal(inv[:, :], sums[:, :]).then_inc(inv_ready, 1)

        def dve_spread(dve, s, g):
            wait_apart(dve, inv_placed, 16 * (NG * s + g) + 16, const_ready)
            nc.vector.stream_shuffle(rs[:, :], rs[:, :], [DH] * 32).then_inc(rs_ready, 1)

        def dve_slot(dve, s, cross, cross_next, prev, nxt):
            for at in range(8 * NG):
                g, j, half = at // 8, at // 2 % GH, at % 2
                tg, ts = (g + 2, s) if g + 2 < NG else (g + 2 - NG, s + 1)
                smax = g + 2 < NG or nxt
                if smax:
                    for qt in (2 * half, 2 * half + 1):
                        dve_smax(dve, ts, tg, j, qt)
                    if at % 8 == 7:
                        dve_parts(dve, ts, tg)
                if at in (2, 3) and nxt:
                    for t in (2 * at - 4, 2 * at - 3):
                        dve_stats(dve, s + 1, t)
                if at == 4 and nxt:
                    dve_stats_end(dve, s + 1)
                for after, step in ((INV, dve_inv), (SPREAD, dve_spread)):
                    group = due(after, at, s, prev)
                    if group:
                        step(dve, *group)
                if 12 <= at < 12 + NT and prev:
                    dve_res(dve, s - 1, at - 12)

        @block.vector
        def _(dve):
            nc.vector.memset(v[:, :, :, DH:DH + 1], 1.0).then_inc(const_ready, 1)
            nc.vector.memset(ps[:, OB, :], 0.0).then_inc(const_ready, 1)
            nc.vector.memset(rs[:, :], 0.0).then_inc(const_ready, 1)
            for t in range(NT):
                dve_stats(dve, 0, t)
            dve_stats_end(dve, 0)
            nc.vector.memset(qs[:, :, :].bitcast(F32), 0.0).then_inc(const_ready, 1)
            nc.vector.memset(ks[:, :, :].bitcast(F32), 0.0).then_inc(const_ready, 1)
            nc.vector.memset(pr[:, 0:3, :, :], 1.0).then_inc(const_ready, 1)
            for g in (0, 1):
                for j in range(GH):
                    for qt in range(NT):
                        dve_smax(dve, 0, g, j, qt)
                dve_parts(dve, 0, g)

            def emit(s, cross, cross_next, prev, nxt):
                dve_slot(dve, s, cross, cross_next, prev, nxt)
            run_slots(dve, emit)
            dve_spread(dve, UNITS - 1, NG - 2)
            dve_inv(dve, UNITS - 1, NG - 1)
            dve_spread(dve, UNITS - 1, NG - 1)
            for t in range(NT):
                dve_res(dve, UNITS - 1, t)

        def pool_norm(pool, u, cross):
            pool.wait_ge(stats_ready, 2 * u + 2)
            nc.gpsimd.tensor_tensor(rstd[:, :], vareps[:, :], neghalf[:, :], ALU.pow).then_inc(rstd_ready, 1)
            pool.wait_ge(rstd_ready, u + 1)
            nc.gpsimd.tensor_tensor(nmr[:, :], negmean[:, :], rstd[:, :], ALU.mult).then_inc(nmr_ready, 1)
            wait_apart(pool, nmr_ready, u + 1, ident_ready)
            for t in range(NT):
                nc.gpsimd.tensor_scalar(xn[:, t, :], xn[:, t, :], rstd[:, t:t + 1], nmr[:, t:t + 1],
                                        ALU.mult, ALU.add).then_inc(xn_ready, 1)

        def pool_split(pool, u, cross, what):
            n = ops_base(u, cross) + ops_of(cross).index(what)
            k = ops_of(cross).index(what)
            pool.wait_ge(op_evac, n + 1)
            if what in ("t2", "c1") or k and ops_of(cross)[k - 1] in ("t2", "c1"):
                pool.wait_ge(op_split, n)
            a = slice(64, P) if what in ("t2", "c1") else slice(0, P)
            one, two = {
                "t0": (h1[:, 0, :], h2[:, 0, :]), "t1": (h1[:, 1, :], h2[:, 1, :]), "t2": (h1[a, 2, :], h1[a, 2, :]),
                "c0": (c1[:, 0, :], c2[:, :]), "c1": (c1[a, 1, :], c1[a, 1, :]),
            }.get(what) or (sq[:, STAGE[what], 0, :], sq[:, STAGE[what], 1, :])
            nc.gpsimd.tensor_tensor(two, whole[a, k % 2, :], one, ALU.subtract).then_inc(op_split, 1)

        def pool_scale(pool, s, g):
            pool.wait_ge(rs_ready, NG * s + g + 1)
            nc.gpsimd.tensor_tensor(on[:, g, :], on[:, g, :], rs[:, :], ALU.mult).then_inc(norm_done, 1)

        def pool_slot(pool, s, cross, cross_next, prev, nxt):
            if prev:
                pool_scale(pool, s - 1, NG - 2)
            if nxt:
                pool_norm(pool, s + 1, cross_next)
            if prev:
                pool_scale(pool, s - 1, NG - 1)
            if cross_next and not cross:
                pool_weights(pool, True)
            if nxt:
                for what in ops_of(cross_next)[:-2]:
                    pool_split(pool, s + 1, cross_next, what)
            pool_scale(pool, s, 0)
            if nxt:
                for what in (QB, KB):
                    pool_split(pool, s + 1, cross_next, what)
            pool_scale(pool, s, 1)
            pool_scale(pool, s, 2)

        @block.gpsimd
        def _(pool):
            nc.gpsimd.memset(ident[:, :], 0.0).then_inc(ident_zero, 1)
            nc.gpsimd.memset(identb[:, :], 0.0).then_inc(ident_zero, 1)
            nc.gpsimd.memset(wo[:, :, :], 0.0).then_inc(ident_zero, 1)
            nc.gpsimd.memset(neghalf[:, :], -0.5).then_inc(ident_zero, 1)
            pool.wait_ge(ident_zero, 4)
            for m in (ident, identb):
                nc.gpsimd.affine_select(out=m[:, :], in_=m[:, :], compare_op=ALU.not_equal, fill=1.0, base=0,
                                        pattern=[[-1, P]], channel_multiplier=1).then_inc(ident_ready, 1)
            pool_norm(pool, 0, False)
            pool_weights(pool, False)
            for what in OPS_SELF:
                pool_split(pool, 0, False, what)

            def emit(s, cross, cross_next, prev, nxt):
                pool_slot(pool, s, cross, cross_next, prev, nxt)
            run_slots(pool, emit)
            for g in (NG - 2, NG - 1):
                pool_scale(pool, UNITS - 1, g)

        def tokens(t, b):
            return t[b].rearrange("(t p) d -> p t d", p=P)

        def sp_stack(sp, u, cross, which, side):
            tile = {0: (QA, KA), 1: (QB, KB), 2: (QKC, QKC)}[which][side]
            pair0, pairs = ((0, 4), (4, 4), (8, 2))[which]
            sp.wait_ge(op_split, op_value(u, cross, tile))
            n = 64 if which < 2 else 32
            first = 64 * side if which == 2 else 0
            for row, *parts in STACK:
                src = sq[:, STAGE[tile], parts[side], :].bitcast(F32)
                if side == 0:
                    sp.dma_start(qs[2 * DH * row:2 * DH * (row + 1), pair0:pair0 + pairs, :].bitcast(F32),
                                 src[first:first + 2 * n, :]).then_inc(stacked[which], 16)
                    continue
                for par in range(2):
                    rows = slice(DH * (2 * row + par), DH * (2 * row + par + 1))
                    sp.dma_start(ks[rows, 2 * pair0 + par:2 * (pair0 + pairs):2, :].bitcast(F32),
                                 src[first + par * n:first + par * n + n, :]).then_inc(stacked[which], 16)

        def sp_max(sp, s, g):
            sp.wait_ge(mt_evac, NG * s + g + 1)
            sp.dma_start(qs[MAX_ROW:MAX_ROW + 4, 2 * g:2 * g + 2, :].bitcast(F32),
                         mt[:, :].bitcast(F32)).then_inc(max_placed, 16)

        def sp_sums(sp, s, g):
            wait_apart(sp, o_evac, NG * s + g + 1, ident_zero)
            if not (isinstance(s, int) and s == 0 and g == 0):
                sp.wait_ge(inv_ready, NG * s + g)
            sp.dma_start(sums[:, :], on[DH:P:32, g, :]).then_inc(sums_spread, 16)

        def sp_inv(sp, s, g):
            if not (isinstance(s, int) and s == 0 and g == 0):
                sp.wait_ge(norm_done, NG * s + g)
            sp.wait_ge(inv_ready, NG * s + g + 1)
            sp.dma_start(rs[DH:P:32, :], inv[:, :]).then_inc(inv_placed, 16)

        def sp_tokens(sp, src):
            sp.dma_start(xn[:, :, 0:D], src).then_inc(xl_loaded, 16)
            sp.dma_start(xn[:, :, D:3 * P], src[:, :, 2 * P:D]).then_inc(xl_loaded, 16)

        def sp_slot(sp, s, cross, cross_next, prev, nxt):
            src = x1 if cross_prev(s, cross) else x
            dst = x2 if cross_prev(s, cross) else x1
            if nxt:
                sp.wait_ge(op_ready, ops_base(s, cross) + 3)
                if cross_next:
                    sp.wait_ge(x_stored, 16 * (s - (B - 2)))
                    sp_tokens(sp, tokens(x1, s - (B - 1)))
                    if cross:
                        sp.wait_ge(op_ready, op_value(s, True, "c1"))
                    src_c = tokens(ctx_in, s - (B - 1))
                    sp.dma_start(cn[:, :, 0:C], src_c).then_inc(cn_loaded, 16)
                    sp.dma_start(cn[:, :, C:2 * P], src_c[:, :, P:C]).then_inc(cn_loaded, 16)
                else:
                    sp_tokens(sp, tokens(x, s + 1))
            if prev:
                if not (isinstance(s, int) and s == 1):
                    sp.wait_ge(x_stored, 16 * (s - 1))
                b = s - 1 - (B if cross_prev(s, cross) else 0)
                sp.dma_start(xr[:, :, :], tokens(src, b)).then_inc(xr_loaded, 16)
            sp_max(sp, s, 1)
            if prev:
                sp_sums(sp, s - 1, NG - 1)
                wait_apart(sp, st_ready, 40 * s, ident_zero)
            sp_stack(sp, s, cross, 2, 0)
            if prev:
                sp_inv(sp, s - 1, NG - 1)
            sp_stack(sp, s, cross, 2, 1)
            if cross_next and not cross:
                sp_weights(sp, True)
            sp_max(sp, s, 2)
            if prev:
                sp.wait_ge(res_done, NT * s)
                sp.dma_start(tokens(dst, b), xr[:, :, :]).then_inc(x_stored, 16)
            if isinstance(s, int) and s == B:
                sp.wait_ge(oproj_ready, NT * B)
                sp_wo(sp, True)
            sp_sums(sp, s, 0)
            if nxt:
                wait_apart(sp, st_ready, 40 * s + 16, ident_zero)
                sp_stack(sp, s + 1, cross_next, 0, 0)
            sp_inv(sp, s, 0)
            if nxt:
                sp_stack(sp, s + 1, cross_next, 0, 1)
            sp_max(sp, s, 3)
            sp_sums(sp, s, 1)
            sp_inv(sp, s, 1)
            sp_max(sp, s, 4)
            sp_sums(sp, s, 2)
            sp_inv(sp, s, 2)
            if nxt:
                wait_apart(sp, st_ready, 40 * s + 32, ident_zero)
                sp_stack(sp, s + 1, cross_next, 1, 0)
                sp_max(sp, s + 1, 0)
            if nxt:
                sp_stack(sp, s + 1, cross_next, 1, 1)
            sp_sums(sp, s, 3)
            sp_inv(sp, s, 3)

        @block.sync
        def _(sp):
            sp_tokens(sp, tokens(x, 0))
            for k, name in enumerate(("n1", "n2")):
                for q, part in enumerate(("_g", "_b")):
                    vec = w[name + part].rearrange("(p a) -> p a", a=1)
                    sp.dma_start(gb[:, k, 0, q:q + 1], vec[0:P]).then_inc(small_loaded, 16)
                    sp.dma_start(gb[:, k, 1, q:q + 1], vec[P:2 * P]).then_inc(small_loaded, 16)
                    sp.dma_start(gb[0:64, k, 2, q:q + 1], vec[2 * P:D]).then_inc(small_loaded, 16)
                    sp.dma_start(gb[64:P, k, 2, q:q + 1], vec[2 * P:D]).then_inc(small_loaded, 16)
            sp_weights(sp, False)
            sp.wait_ge(ident_zero, 4)
            sp_wo(sp, False)
            sp.wait_ge(const_ready, 6)
            ones = pr[0:2, 0:3, :, :].rearrange("p a b c -> p (a b c)")[:, 0:(H // 2) * N]
            for par in range(2):
                first = MAX_ROW + 2 * par
                sp.dma_start(ks[first:first + 2, par:H:2, :].bitcast(F32),
                             ones.rearrange("p (h n) -> p h n", n=N)).then_inc(ones_loaded, 16)
            for which in (0, 1):
                for side in (0, 1):
                    sp_stack(sp, 0, False, which, side)
            sp_max(sp, 0, 0)

            def emit(s, cross, cross_next, prev, nxt):
                sp_slot(sp, s, cross, cross_next, prev, nxt)
            run_slots(sp, emit)
            u = UNITS - 1
            sp_sums(sp, u, NG - 1)
            sp_inv(sp, u, NG - 1)
            sp.wait_ge(x_stored, 16 * u)
            sp.dma_start(xr[:, :, :], tokens(x1, B - 1)).then_inc(xr_loaded, 16)
            sp.wait_ge(res_done, NT * UNITS)
            sp.dma_start(tokens(x2, B - 1), xr[:, :, :]).then_inc(x_stored, 16)
            sp.wait_ge(x_stored, 16 * UNITS)


def feed_forward(nc, x2, w, out):
    with ExitStack() as ctx:
        def sb(name, shape, dt=F32):
            return ctx.enter_context(nc.sbuf_tensor("ff_" + name, shape, dt))

        def sem(name):
            return ctx.enter_context(nc.semaphore("ff_" + name))

        ps = ctx.enter_context(nc.psum_tensor("ff_ps", [P, 8, 512], F32))
        ACC, AG = 0, 4

        xl = sb("xl", [P, NT, D])
        xr = sb("xr", [P, NT, D])
        y = sb("y", [P, NT, D])
        xn = sb("xn", [P, NT, 3 * P])
        mv6 = sb("mv6", [P, NT, 6])
        mv = sb("mv", [P, NT, 2])
        negmean = sb("negmean", [P, NT])
        vareps = sb("vareps", [P, NT])
        rstd = sb("rstd", [P, NT])
        nmr = sb("nmr", [P, NT])
        neghalf = sb("neghalf", [P, NT])
        gb = sb("gb", [P, 3, 2])
        b1 = sb("b1", [P, 2 * MC])
        b2 = sb("b2", [P, D])
        h1 = sb("h1", [P, 3, N], F32R)
        h2 = sb("h2", [P, 2, N], F32R)
        whole = sb("whole", [P, 3, N])
        gate = sb("gate", [P, 2, N])
        u = sb("u", [P, 3, N])
        u1 = sb("u1", [P, 3, N], F32R)
        u2 = sb("u2", [P, 3, N], F32R)
        raw = sb("raw", [P, 2, 2 * F])
        wa1 = sb("wa1", [P, 3, 2 * F], F32R)
        wa2 = sb("wa2", [P, 3, 2 * F], F32R)
        wb1 = sb("wb1", [P, MC, D], F32R)
        wb2 = sb("wb2", [P, MC, D], F32R)
        ident = sb("ident", [P, P])

        ident_zero = sem("ident_zero")
        ident_ready = sem("ident_ready")
        small_loaded = sem("small_loaded")
        raw_loaded = [sem("raw_loaded0"), sem("raw_loaded1")]
        raw_rounded = sem("raw_rounded")
        raw_split = sem("raw_split")
        xl_loaded = sem("xl_loaded")
        xr_loaded = sem("xr_loaded")
        y_stored = sem("y_stored")
        stats_raw = sem("stats_raw")
        stats_mv = sem("stats_mv")
        stats_ready = sem("stats_ready")
        rstd_ready = sem("rstd_ready")
        nmr_ready = sem("nmr_ready")
        xn_ready = sem("xn_ready")
        t_ready = sem("t_ready")
        t_evac = sem("t_evac")
        t_split = sem("t_split")
        ag_ready = sem("ag_ready")
        gate_ready = sem("gate_ready")
        u_ready = sem("u_ready")
        u1_ready = sem("u1_ready")
        u2_ready = sem("u2_ready")
        acc_ready = sem("acc_ready")
        y_ready = sem("y_ready")
        b2_added = sem("b2_added")

        RAW_FULL = [16, 16, 48, 32, 64]
        HALF = MC // 2

        def raw_tile(i):
            return raw[:, i % 2, :] if i < 3 else raw[:, i % 2, 0:HALF * D].rearrange("p (f n) -> p f n", n=D)

        def parts_of(i):
            if i < 3:
                return wa1[:, i, :], wa2[:, i, :]
            f = slice((i - 3) * HALF, (i - 2) * HALF)
            return wb1[:, f, :], wb2[:, f, :]

        def each_batch(eng, emit):
            emit(0, True)
            with eng.Fori(1, B - 1) as b:
                emit(b, True)
            emit(B - 1, False)

        block = ctx.enter_context(nc.Block())

        def tokens(t, b):
            return t[b].rearrange("(t p) d -> p t d", p=P)

        @block.sync
        def _(sp):
            sp.dma_start(xl[:, :, :], tokens(x2, 0)).then_inc(xl_loaded, 16)
            for q, part in enumerate(("n3_g", "n3_b")):
                vec = w[part].rearrange("(p a) -> p a", a=1)
                sp.dma_start(gb[:, 0, q:q + 1], vec[0:P]).then_inc(small_loaded, 16)
                sp.dma_start(gb[:, 1, q:q + 1], vec[P:2 * P]).then_inc(small_loaded, 16)
                sp.dma_start(gb[0:64, 2, q:q + 1], vec[2 * P:D]).then_inc(small_loaded, 16)
                sp.dma_start(gb[64:P, 2, q:q + 1], vec[2 * P:D]).then_inc(small_loaded, 16)
            for i in range(5):
                if i >= 2:
                    sp.wait_ge(raw_split, i - 1)
                if i < 3:
                    n = chunk_rows(D, i)
                    for at in range(0, P, n):
                        sp.dma_start(raw[at:at + n, i % 2, :], w["ff_w1"][i * P:i * P + n, :])\
                          .then_inc(raw_loaded[i % 2], 16)
                else:
                    sp.dma_start(raw_tile(i), w["ff_w2"].rearrange("(f p) n -> p f n", p=P)
                                 [:, (i - 3) * HALF:(i - 2) * HALF, :]).then_inc(raw_loaded[i % 2], 16)
                if i == 1:
                    sp.dma_start(b1[:, :], w["ff_b1"].rearrange("(c p) -> p c", p=P),
                                 allow_slow_non_contiguous=True).then_inc(small_loaded, 16)
                    sp.dma_start(b2[:, :], w["ff_b2"].rearrange("(a n) -> a n", a=1).broadcast_to([P, D]))\
                      .then_inc(small_loaded, 16)

            def emit(b, nxt):
                if nxt:
                    sp.wait_ge(xn_ready, 2 * NT * b + 2 * NT)
                    sp.dma_start(xl[:, :, :], tokens(x2, b + 1)).then_inc(xl_loaded, 16)
                sp.wait_ge(y_ready, NT * b)
                sp.dma_start(xr[:, :, :], tokens(x2, b)).then_inc(xr_loaded, 16)
                sp.wait_ge(y_ready, NT * b + NT)
                sp.dma_start(tokens(out, b), y[:, :, :]).then_inc(y_stored, 16)
            each_batch(sp, emit)
            sp.wait_ge(y_stored, 16 * B)

        @block.tensor
        def _(pe):
            def transposes(b, waits):
                pe.wait_ge(xn_ready, 2 * NT * b + 2 * NT)
                for c, (bank, free) in enumerate(zip((AG, AG + 1, AG + 2), waits)):
                    if free is not None:
                        pe.wait_ge(u_ready, free)
                    for t in range(NT):
                        ins = nc.tensor.transpose(ps[:, bank, t * P:t * P + P], xn[:, t, c * P:c * P + P], ident[:, :])
                    ins.then_inc(t_ready, 1)

            def pair(b, f):
                if f == 0:
                    pe.wait_ge(t_split, 3 * b + 3)
                elif f == 1:
                    pe.wait_ge(u_ready, MC * b)
                else:
                    pe.wait_ge(u_ready, MC * b + f - 1)
                for side in (1, 0):
                    cols = slice(side * F + f * P, side * F + f * P + P)
                    todo = ([(wa1[:, c, cols], h1[:, c, :]) for c in range(3)]
                            + [(wa2[:, c, cols], h1[:, c, :]) for c in range(2)]
                            + [(wa2[0:64, 2, cols], h1[0:64, 2, :])]
                            + [(wa1[:, c, cols], h2[:, c, :]) for c in range(2)])
                    for n, (wt, d) in enumerate(todo):
                        ins = nc.tensor.matmul(ps[:, AG + 2 * (f % 2) + side, :], wt, d,
                                               start=(n == 0), stop=(n == len(todo) - 1))
                    ins.then_inc(ag_ready, 1)

            def down(b, f):
                if f == 0:
                    pe.wait_ge(y_ready, NT * b)
                pe.wait_ge(u1_ready, MC * b + f + 1)
                for t in range(NT):
                    toks = slice(t * P, t * P + P)
                    nc.tensor.matmul(ps[:, ACC + t, 0:D], u1[:, f % 3, toks], wb1[:, f, :], start=(f == 0), stop=False)
                    ins = nc.tensor.matmul(ps[:, ACC + t, 0:D], u1[:, f % 3, toks], wb2[:, f, :], start=False, stop=False)
                pe.wait_ge(u2_ready, MC * b + f + 1)
                for t in range(NT):
                    toks = slice(t * P, t * P + P)
                    ins = nc.tensor.matmul(ps[:, ACC + t, 0:D], u2[:, f % 3, toks], wb1[:, f, :],
                                           start=False, stop=(f == MC - 1))
                    if f == MC - 1:
                        ins.then_inc(acc_ready, 1)

            pe.wait_ge(ident_ready, 1)
            transposes(0, (None, None, None))
            pe.wait_ge(raw_split, 5)

            def emit(b, nxt):
                for f in range(MC):
                    pair(b, f)
                    if f >= 2:
                        down(b, f - 2)
                if nxt:
                    at = MC * b + MC
                    transposes(b + 1, (at - 1, at - 1, at))
                down(b, MC - 2)
                down(b, MC - 1)
            each_batch(pe, emit)

        @block.scalar
        def _(act):
            def features(b):
                for c in range(3):
                    act.wait_ge(t_ready, 3 * b + c + 1)
                    if c == 0 and not (isinstance(b, int) and b == 0):
                        act.wait_ge(t_split, 3 * b)
                    kw = dict(scale=gb[:, c, 0:1], bias=gb[:, c, 1:2])
                    nc.scalar.activation(h1[:, c, :], ps[:, AG + c, :], ACT.Identity, **kw)
                    nc.scalar.activation(whole[:, c, :], ps[:, AG + c, :], ACT.Identity, **kw).then_inc(t_evac, 1)

            act.wait_ge(small_loaded, 16 * 10)
            for i in range(5):
                act.wait_ge(raw_loaded[i % 2], RAW_FULL[i])
                nc.scalar.activation(parts_of(i)[0], raw_tile(i), ACT.Copy).then_inc(raw_rounded, 1)
                if i == 1:
                    features(0)

            def rounded(b, f):
                act.wait_ge(u_ready, MC * b + f + 1)
                nc.scalar.activation(u1[:, f % 3, :], u[:, f % 3, :], ACT.Copy).then_inc(u1_ready, 1)

            def emit(b, nxt):
                for f in range(MC):
                    act.wait_ge(ag_ready, 2 * MC * b + 2 * f + 1)
                    if f < 2:
                        act.wait_ge(u_ready, MC * b)
                    nc.scalar.activation(gate[:, f % 2, :], ps[:, AG + 2 * (f % 2) + 1, :], ACT.Gelu,
                                         bias=b1[:, MC + f:MC + f + 1]).then_inc(gate_ready, 1)
                    if f:
                        rounded(b, f - 1)
                rounded(b, MC - 1)
                if nxt:
                    features(b + 1)
            each_batch(act, emit)

        @block.vector
        def _(dve):
            def stats(b):
                dve.wait_ge(xl_loaded, 16 * b + 16)
                for t in range(NT):
                    nc.vector.bn_stats(mv6[:, t, :], xl[:, t, :]).then_inc(stats_raw, 1)
                wait_apart(dve, nmr_ready, b, xl_loaded)
                wait_apart(dve, stats_raw, NT * b + NT, xl_loaded)
                for t in range(NT):
                    nc.vector.bn_aggr(mv[:, t, :], mv6[:, t, :]).then_inc(stats_mv, 1)
                dve.wait_ge(stats_mv, NT * b + NT)
                nc.vector.tensor_scalar(negmean[:, :], mv[:, :, 0], -1.0, None, ALU.mult).then_inc(stats_ready, 1)
                nc.vector.tensor_scalar(vareps[:, :], mv[:, :, 1], EPS, None, ALU.add).then_inc(stats_ready, 1)

            stats(0)
            for i in range(5):
                dve.wait_ge(raw_rounded, i + 1)
                one, two = parts_of(i)
                nc.vector.tensor_tensor(two, raw_tile(i), one, ALU.subtract).then_inc(raw_split, 1)

            def emit(b, nxt):
                for f in range(MC):
                    dve.wait_ge(ag_ready, 2 * MC * b + 2 * f + 2)
                    dve.wait_ge(gate_ready, MC * b + f + 1)
                    if f < 3:
                        dve.wait_ge(u2_ready, MC * b)
                    else:
                        dve.wait_ge(u2_ready, MC * b + f - 2)
                    nc.vector.scalar_tensor_tensor(out=u[:, f % 3, :], in0=ps[:, AG + 2 * (f % 2), :],
                                                   scalar=b1[:, f:f + 1], in1=gate[:, f % 2, :],
                                                   op0=ALU.add, op1=ALU.mult).then_inc(u_ready, 1)
                    if f == 1 and nxt:
                        stats(b + 1)
                dve.wait_ge(b2_added, NT * b + NT)
                dve.wait_ge(y_stored, 16 * b)
                for t in range(NT):
                    dve.wait_ge(acc_ready, NT * b + t + 1)
                    nc.vector.tensor_tensor(y[:, t, :], ps[:, ACC + t, 0:D], xr[:, t, :], ALU.add).then_inc(y_ready, 1)
            each_batch(dve, emit)

        @block.gpsimd
        def _(pool):
            nc.gpsimd.memset(ident[:, :], 0.0).then_inc(ident_zero, 1)
            nc.gpsimd.memset(neghalf[:, :], -0.5).then_inc(ident_zero, 1)
            pool.wait_ge(ident_zero, 2)
            nc.gpsimd.affine_select(out=ident[:, :], in_=ident[:, :], compare_op=ALU.not_equal, fill=1.0, base=0,
                                    pattern=[[-1, P]], channel_multiplier=1).then_inc(ident_ready, 1)

            def norm(b):
                pool.wait_ge(stats_ready, 2 * b + 2)
                nc.gpsimd.tensor_tensor(rstd[:, :], vareps[:, :], neghalf[:, :], ALU.pow).then_inc(rstd_ready, 1)
                pool.wait_ge(rstd_ready, b + 1)
                nc.gpsimd.tensor_tensor(nmr[:, :], negmean[:, :], rstd[:, :], ALU.mult).then_inc(nmr_ready, 1)
                wait_apart(pool, nmr_ready, b + 1, ident_ready)
                wait_apart(pool, t_ready, 3 * b, ident_ready)
                for t in range(NT):
                    for a, e in ((0, D), (2 * P, D)):
                        to = a if a == 0 else D
                        nc.gpsimd.tensor_scalar(xn[:, t, to:to + e - a], xl[:, t, a:e], rstd[:, t:t + 1],
                                                nmr[:, t:t + 1], ALU.mult, ALU.add).then_inc(xn_ready, 1)

            def features(b):
                for c in range(3):
                    pool.wait_ge(t_evac, 3 * b + c + 1)
                    if c == 2:
                        pool.wait_ge(t_split, 3 * b + 2)
                    a = slice(64, P) if c == 2 else slice(0, P)
                    two = h1[a, 2, :] if c == 2 else h2[:, c, :]
                    nc.gpsimd.tensor_tensor(two, whole[a, c, :], h1[a, c, :], ALU.subtract).then_inc(t_split, 1)
                pool.wait_ge(t_split, 3 * b + 3)

            norm(0)
            features(0)
            pool.wait_ge(small_loaded, 16 * 10)

            def emit(b, nxt):
                for f in range(MC):
                    pool.wait_ge(u1_ready, MC * b + f + 1)
                    nc.gpsimd.tensor_tensor(u2[:, f % 3, :], u[:, f % 3, :], u1[:, f % 3, :],
                                            ALU.subtract).then_inc(u2_ready, 1)
                    if f == 2 and nxt:
                        norm(b + 1)
                    if f == 4:
                        pool.wait_ge(xr_loaded, 16 * b + 16)
                        for t in range(NT):
                            nc.gpsimd.tensor_tensor(xr[:, t, :], xr[:, t, :], b2[:, :], ALU.add).then_inc(b2_added, 1)
                if nxt:
                    features(b + 1)
            each_batch(pool, emit)


def layer(nc, x, ctx_in, w, out):
    x1 = nc.dram_tensor("x_after_self", [B, N, D], F32).ap()
    x2 = nc.dram_tensor("x_after_cross", [B, N, D], F32).ap()
    attention(nc, x, ctx_in, w, x1, x2)
    feed_forward(nc, x2, w, out)


_WEIGHTS = ["n1_g", "n1_b", "q1", "k1", "v1", "o1_w", "o1_b", "n2_g", "n2_b", "q2", "k2", "v2", "o2_w", "o2_b",
            "n3_g", "n3_b", "ff_w1", "ff_b1", "ff_w2", "ff_b2"]


def kernel(**inputs):
    import numpy as _np
    import concourse.bacc as _bacc
    from concourse import mybir as _mybir
    from concourse.bass_utils import run_bass_kernel_spmd as _run

    nc = _bacc.Bacc("TRN2", target_bir_lowering=False, num_devices=1)
    arrays, aps = {}, {}
    for name in ["x", "ctx_768"] + ["L0_xattn_" + n for n in _WEIGHTS]:
        a = _np.ascontiguousarray(inputs[name])
        arrays[f"in_{name}_dram"] = a
        aps[name] = nc.dram_tensor(f"in_{name}_dram", a.shape, _mybir.dt.from_np(a.dtype), kind="ExternalInput").ap()
    out = nc.dram_tensor("out_0_dram", (B, N, D), _mybir.dt.float32, kind="ExternalOutput").ap()
    layer(nc, aps["x"], aps["ctx_768"], {n: aps["L0_xattn_" + n] for n in _WEIGHTS}, out)
    r = _run(nc, [arrays], core_ids=[0])
    return r.results[0]["out_0_dram"]
```

```python
from contextlib import ExitStack

import concourse.bass as bass
from concourse import mybir

F32 = mybir.dt.float32
F32R = mybir.dt.float32r
BF16 = mybir.dt.bfloat16
ALU = mybir.AluOpType
ACT = mybir.ActivationFunctionType
AX_X = mybir.AxisListType.X

P = 128
B, N, D, C = 8, 512, 320, 192
H, DH = 20, 16
F = 1280
EPS = 1e-5
SCALE = DH ** -0.5
NT = N // P
GH = 4
NG = H // GH
UNITS = 2 * B
MAX_ROW = 96
MC = F // P

QA, KA, QKC, QB, KB = range(5)
STACK = [(0, 0, 0), (1, 1, 0), (2, 0, 1)]
STACK_DMAS = 16 * 3 * (1 + 2)
STAGE = [0, 1, 2, 0, 1]
RING = 5

OPS_SELF = ["t0", "t1", "t2", QA, KA, QKC, QB, KB]
OPS_CROSS = ["t0", "t1", "t2", QA, "c0", "c1", KA, QKC, QB, KB]


def ops_of(cross):
    return OPS_CROSS if cross else OPS_SELF


def ops_base(u, cross):
    return 10 * u - 2 * B if cross else 8 * u


def chunk_rows(width, c):
    return min(P, width - c * P)


def wait_apart(eng, sem, value, passed):
    if not isinstance(value, int):
        eng.lower_val(value)
    eng.wait_ge(passed, 1)
    eng.wait_ge(sem, value)


def shared_place(nc, outer, early, late):
    with ExitStack() as first:
        got_early = [first.enter_context(nc.sbuf_tensor(*t)) for t in early]
    return got_early, [outer.enter_context(nc.sbuf_tensor(*t)) for t in late]


def attention(nc, x, ctx_in, w, x1, x2, outer):
    (qs, ks), (wa1, wa2) = shared_place(nc, outer, [
        ("qs", [P, H // 2, N], F32R),
        ("ks", [P, H, N], F32R),
    ], [("wa1", [P, 3, 2 * F], F32R), ("wa2", [P, 3, 2 * F], F32R)])
    (pr,), (wb1, wb2) = shared_place(nc, outer, [("pr", [P, RING, NT, N], F32)],
                                     [("wb1", [P, MC, D], F32R), ("wb2", [P, MC, D], F32R)])
    with ExitStack() as ctx:
        def sb(name, shape, dt=F32):
            return ctx.enter_context(nc.sbuf_tensor(name, shape, dt))

        sb("rest_of_pr", [P, RING * NT * N - 2 * MC * D])
        (h1, c1, wqk1, wqk2, wv1, wv2, sq), (ff_raw1, ff_raw2, _) = shared_place(nc, ctx, [
            ("h1", [P, 3, N], F32R),
            ("c1", [P, 2, N], F32R),
            ("wqk1", [P, 3, 5, P], F32R), ("wqk2", [P, 3, 5, P], F32R),
            ("wv1", [P, 3, D], F32R), ("wv2", [P, 3, D], F32R),
            ("sq", [P, 3, 2, N], F32R),
        ], [("ff_raw1", [P, 3, 2 * F], F32), ("ff_raw2", [P, MC, D], F32), ("rest_of_sq", [P, 512], F32)])

        def sem(name):
            return ctx.enter_context(nc.semaphore(name))

        ps = ctx.enter_context(nc.psum_tensor("ps", [P, 8, 512], F32))
        ST, SM, OB, DB = 0, 4, 6, 7

        xn = sb("xn", [P, NT, D])
        xr = sb("xr", [P, NT, D])
        cn = sb("cn", [P, NT, 2 * P])
        mv6 = sb("mv6", [P, NT, 6])
        mv = sb("mv", [P, NT, 2])
        small = sb("small", [P, 6, NT])
        negmean, vareps, rstd, nmr, neghalf, second = (small[:, k, :] for k in range(6))
        gb = sb("gb", [P, 2, 3, 2])
        h2 = sb("h2", [P, 2, N], F32R)
        c2 = sb("c2", [P, N], F32R)
        whole = sb("whole", [P, 2, N])
        raw = sb("raw", [P, D])
        wo1 = sb("wo1", [P, NG, D], F32R)
        wo2 = sb("wo2", [P, NG, D], F32R)
        v = sb("v", [P, NT, H, DH + 1])
        on = sb("on", [P, 2, N])
        ons = sb("ons", [P, NG, N], F32R)
        sums = sb("sums", [P, GH * N // P])
        inv = sb("inv", [P, GH * N // P])
        rs = sb("rs", [P, N])
        nm = sb("nm", [P, NT, 2, 2])
        mh = sb("mh", [P, NT, 2, 2, 2], BF16)
        rows = sb("rows", [P, 2 * D + P], F32R)
        ident = sb("ident", [P, P])
        identb = sb("identb", [P, P], BF16)

        const_ready = sem("const_ready")
        ident_zero = sem("ident_zero")
        ident_ready = sem("ident_ready")
        ones_loaded = sem("ones_loaded")
        small_loaded = [sem("norm1_loaded"), sem("norm2_loaded")]
        wo_loaded = sem("wo_loaded")
        wo_rounded = sem("wo_rounded")
        wo_split = sem("wo_split")
        bias_loaded = sem("bias_loaded")
        bias_rounded = sem("bias_rounded")
        bias_split = sem("bias_split")
        second_ready = sem("second_ready")
        raw_loaded = [sem(f"raw_loaded{i}") for i in range(9)]
        raw_split = sem("raw_split")
        w_rounded = sem("w_rounded")
        w_zeroed = sem("w_zeroed")
        xl_loaded = sem("xl_loaded")
        cn_loaded = sem("cn_loaded")
        xr_loaded = sem("xr_loaded")
        x_stored = sem("x_stored")
        stats_raw = sem("stats_raw")
        stats_mv = sem("stats_mv")
        stats_ready = sem("stats_ready")
        rstd_ready = sem("rstd_ready")
        nmr_ready = sem("nmr_ready")
        xn_ready = sem("xn_ready")
        op_ready = sem("op_ready")
        op_evac = sem("op_evac")
        op_split = sem("op_split")
        v_ready = sem("v_ready")
        v_evac = sem("v_evac")
        stacked = [sem("stacked_a"), sem("stacked_b"), sem("stacked_c")]
        smax_ready = sem("smax_ready")
        smax_free = sem("smax_free")
        mh_ready = sem("mh_ready")
        mt_ready = sem("mt_ready")
        mt_evac = sem("mt_evac")
        max_placed = sem("max_placed")
        st_ready = sem("st_ready")
        exp_done = sem("exp_done")
        o_ready = sem("o_ready")
        o_evac = sem("o_evac")
        sums_spread = sem("sums_spread")
        inv_ready = sem("inv_ready")
        inv_placed = sem("inv_placed")
        rs_ready = sem("rs_ready")
        mh_high = sem("mh_high")
        scaled = sem("scaled")
        norm_rounded = sem("norm_rounded")
        norm_done = sem("norm_done")
        oproj_ready = sem("oproj_ready")
        res_done = sem("res_done")
        ff_loaded = [sem(f"ff_loaded{i}") for i in range(4)]
        ff_rounded = sem("ff_rounded")
        ff_split = sem("ff_split")

        FF_PIECES = [(ff_raw1[:, c, :], wa1[:, c, :], wa2[:, c, :]) for c in range(3)] + \
                    [(ff_raw2[:, :, :], wb1[:, :, :], wb2[:, :, :])]
        FF_FULL = [16, 16, 32, 16]

        def sp_ff_weights(sp, i):
            if i == 0:
                sp.wait_ge(v_ready, NT * UNITS)
                sp.wait_ge(stacked[2], STACK_DMAS * UNITS)
            if i == 3:
                sp.dma_start(ff_raw2[:, :, :], w["ff_w2"].rearrange("(f p) n -> p f n", p=P)).then_inc(ff_loaded[i], 16)
                return
            n = chunk_rows(D, i)
            for at in range(0, P, n):
                sp.dma_start(ff_raw1[at:at + n, i, :], w["ff_w1"][i * P:i * P + n, :]).then_inc(ff_loaded[i], 16)

        def act_ff_weights(act, i):
            act.wait_ge(ff_loaded[i], FF_FULL[i])
            raw_i, one, _ = FF_PIECES[i]
            nc.scalar.activation(one, raw_i, ACT.Copy).then_inc(ff_rounded, 1)

        def split_ff_weights(eng, ops, i):
            eng.wait_ge(ff_rounded, i + 1)
            raw_i, one, two = FF_PIECES[i]
            ops.tensor_tensor(two, raw_i, one, ALU.subtract).then_inc(ff_split, 1)

        def weight_chunks(cross):
            pre = "2" if cross else "1"
            wide = C if cross else D
            return ([("q" + pre, D, c) for c in range(3)] + [("k" + pre, wide, c) for c in range((wide + P - 1) // P)]
                    + [("v" + pre, wide, c) for c in range((wide + P - 1) // P)])

        def weight_pieces(name, c):
            out = []
            if name[0] == "v":
                return [(lambda t: t[0][:, c, :], "v", lambda r: r)]
            first = {"q": 0, "k": 1}[name[0]]
            for tile, h0, nh in ((QA + first, 0, 8), (QB + first, 8, 8), (QKC, 16, 4)):
                def dst(wt, tile=tile, nh=nh):
                    if name == "k2" and nh == 4:
                        a = wt[:, 2, (KA, KB)[c], 64:128]
                    elif nh == 4:
                        a = wt[:, c, tile, 64 * first:64 * first + 64]
                    else:
                        a = wt[:, c, tile, :]
                    return a.rearrange("p (r d h) -> p r d h", r=2, d=DH)

                def src_of(r, h0=h0, nh=nh):
                    return r[:, DH * h0:DH * (h0 + nh)].rearrange("p (h r d) -> p r d h", r=2, d=DH)
                out.append((dst, "qk", src_of))
            return out

        SELF_CHUNKS, CROSS_CHUNKS = len(weight_chunks(False)), len(weight_chunks(True))
        QK_CHUNKS = {False: 6, True: 5}
        pieces_before = {False: 0, True: sum(len(weight_pieces(n, c)) for n, _, c in weight_chunks(False))}

        flat_pr = pr[:, :, :, :].rearrange("p a b c -> p (a b c)")
        ONES = H // 2 * N
        RAW0 = ONES
        RAW_WO = RAW0 + SELF_CHUNKS * D
        RAW_BIAS = RAW_WO + NG * D
        IN_CN = NT * 2 * P // D

        def raw_at(cross, i):
            if not cross:
                return flat_pr[:, RAW0 + i * D:RAW0 + i * D + D]
            if i >= IN_CN:
                return raw[:, :]
            return cn[:, :, :].rearrange("p t n -> p (t n)")[:, i * D:i * D + D]

        def sp_weights(sp, cross, chunks):
            for i in chunks:
                name, wide, c = weight_chunks(cross)[i]
                if cross and i > IN_CN:
                    sp.wait_ge(raw_split, SELF_CHUNKS + i)
                n = chunk_rows(wide, c)
                for at in range(0, P, n):
                    sp.dma_start(raw_at(cross, i)[at:at + n, :], w[name][c * P:c * P + n, :]).then_inc(raw_loaded[i], 16)

        def raw_full(cross, i):
            plans = [weight_chunks(False)] + ([weight_chunks(True)] if cross else [])
            return sum(16 * (P // chunk_rows(*plan[i][1:])) for plan in plans)

        def act_weights(act, cross, chunks):
            for i in chunks:
                name, _, c = weight_chunks(cross)[i]
                act.wait_ge(raw_loaded[i], raw_full(cross, i))
                for dst, kind, src in weight_pieces(name, c):
                    to = wv1[:, c, :] if kind == "v" else dst(wqk1)
                    nc.scalar.activation(to, src(raw_at(cross, i)), ACT.Copy).then_inc(w_rounded, 1)

        def split_weights(eng, ops, cross, chunks):
            done = pieces_before[cross] + sum(len(weight_pieces(n, c)) for n, _, c in weight_chunks(cross)[:chunks[0]])
            for i in chunks:
                name, _, c = weight_chunks(cross)[i]
                for dst, kind, src in weight_pieces(name, c):
                    done += 1
                    eng.wait_ge(w_rounded, done)
                    one = wv1[:, c, :] if kind == "v" else dst(wqk1)
                    two = wv2[:, c, :] if kind == "v" else dst(wqk2)
                    ins = ops.tensor_tensor(two, src(raw_at(cross, i)), one, ALU.subtract)
                ins.then_inc(raw_split, 1)

        def pool_zero_halves(pool):
            for wt in (wqk1, wqk2):
                nc.gpsimd.memset(wt[:, :, QKC, 64:128].bitcast(F32), 0.0).then_inc(w_zeroed, 1)
                nc.gpsimd.memset(wt[:, 2, 1:5:3, 0:64].bitcast(F32), 0.0).then_inc(w_zeroed, 1)
            pool.wait_ge(w_zeroed, 4)

        def wo_pieces(cross):
            if cross:
                return [(xr[:, :, :], slice(0, NT)), (raw[:, :].rearrange("p (g n) -> p g n", g=1), slice(NT, NG))]
            return [(flat_pr[:, RAW_WO:RAW_BIAS].rearrange("p (g n) -> p g n", g=NG), slice(0, NG))]

        def sp_wo(sp, cross):
            src = w["o2_w" if cross else "o1_w"].rearrange("(g j d) n -> j d g n", j=GH, d=DH)
            for raw_wo, groups in wo_pieces(cross):
                for block in range(2 * GH):
                    sp.dma_start(raw_wo[DH * block:DH * (block + 1), :, :],
                                 src[block // 2][:, groups, :]).then_inc(wo_loaded, 16)

        def act_wo(act, cross):
            act.wait_ge(wo_loaded, 16 * 2 * GH * (3 if cross else 1))
            for raw_wo, groups in wo_pieces(cross):
                nc.scalar.activation(wo1[:, groups, :], raw_wo, ACT.Copy).then_inc(wo_rounded, 1)

        def dve_wo(dve, cross):
            dve.wait_ge(wo_rounded, 3 if cross else 1)
            for raw_wo, groups in wo_pieces(cross):
                nc.vector.tensor_tensor(wo2[:, groups, :], raw_wo, wo1[:, groups, :], ALU.subtract).then_inc(wo_split, 1)

        def products(w1, w2, d1, d2, chunks):
            full = chunks - 1
            return ([(w1(c), d1(c)) for c in range(full)] + [(w2(c), d1(c)) for c in range(full)]
                    + [(w1(full), d1(full)), (w2(full, 64), d1(full, 64))] + [(w1(c), d2(c)) for c in range(full)])

        def tile_products(tile, cross):
            def part(wt, k, chunk=lambda c: c):
                return lambda c, n=P: wt[0:n, chunk(c), k(c) if callable(k) else k, :]
            on_h = (lambda c, n=P: h1[0:n, c, :], lambda c: h2[:, c, :], 3)
            on_c = (lambda c, n=P: c1[0:n, c, :], lambda c: c2[:, :], 2)
            if not cross or tile in (QA, QB):
                return products(part(wqk1, tile), part(wqk2, tile), *on_h)
            if tile in (KA, KB):
                return products(part(wqk1, tile), part(wqk2, tile), *on_c)
            return (products(part(wqk1, QKC), part(wqk2, QKC), *on_h)
                    + products(part(wqk1, lambda c: (KA, KB)[c], lambda c: 2),
                               part(wqk2, lambda c: (KA, KB)[c], lambda c: 2), *on_c))

        def value_products(t, cross):
            toks = slice(t * P, t * P + P)
            d1, d2, n = ((lambda c, n=P: c1[0:n, c, toks], lambda c: c2[:, toks], 2) if cross
                         else (lambda c, n=P: h1[0:n, c, toks], lambda c: h2[:, c, toks], 3))
            got = products(lambda c, n=P: wv1[0:n, c, :], lambda c, n=P: wv2[0:n, c, :], d1, d2, n)
            return [(d, wt) for wt, d in got]

        def dense_plan(cross_next):
            plan = {2: ("mt", 0), 11: ("mt", 1), 20: ("mt", 2), 26: ("mt", 3), 34: ("mt", 4)}
            plan.update({4 + t: ("v", t) for t in range(NT)})
            plan.update({8 + c: ("op", f"t{c}") for c in range(3)})
            plan.update({12 + t: ("o", t) for t in range(NT)})
            plan.update({16: ("op", QA), 21: ("op", QKC), 25: ("op", QB), 28: ("op", KB)})
            plan.update({17: ("op", "c0"), 18: ("op", "c1"), 19: ("op", KA)} if cross_next else {18: ("op", KA)})
            return plan

        EVAC = [15, 12, 12, 12, 12]
        INV = [18, 16, 16, 16, 14]
        SPREAD = [21, 18, 18, 19, 16]
        ROUND = [23, 21, 21, 21, 17]
        REST = [24, 23, 23, 22, 18]

        WEIGHTS_AT = [0, 1, 2, 3, 10, 16, 24]

        def due(after, at, s, prev):
            for g in range(NG):
                if 8 * g + after[g] == at:
                    return s, g
                if 8 * g + after[g] == at + 8 * NG and prev:
                    return s - 1, g
            return None

        def has(kind, what, g, s_prev, s_next):
            if kind == "op":
                return s_next
            if kind == "o":
                return s_prev
            if kind == "mt":
                return s_next or what + 1 < NG
            return True

        def pe_free_wait(pe, last):
            if last is not None:
                pe.wait_ge(*last)

        def pe_smax(pe, s, g, j, qts):
            h = GH * g + j
            if j == 0 and 0 in qts:
                pe.wait_ge(stacked[(0, 0, 1, 1, 2)[g]], STACK_DMAS * (s + 1))
            for qt in qts:
                pe.wait_ge(smax_free, 80 * s + 4 * h + qt + 1)
                nc.tensor.matmul(ps[:, SM + qt % 2, :], qs[0:MAX_ROW, h // 2, qt * P:qt * P + P],
                                 ks[0:MAX_ROW, h, :], start=True, stop=True).then_inc(smax_ready, 1)

        def pe_st(pe, s, g, j, pair):
            h = GH * g + j
            if j == 0 and pair == 0:
                pe.wait_ge(max_placed, 16 * (NG * s + g) + 16)
            pe.wait_ge(exp_done, 40 * s + 2 * h + pair + 1)
            for kt in (2 * pair, 2 * pair + 1):
                ins = nc.tensor.matmul(ps[:, ST + kt, :], ks[:, h, kt * P:kt * P + P],
                                       qs[:, h // 2, :], start=True, stop=True)
            ins.then_inc(st_ready, 1)

        def pe_pv(pe, s, g, kt):
            if kt == 0:
                if not (isinstance(s, int) and s == 0 and g == 0):
                    pe.wait_ge(o_evac, NG * s + g)
                pe.wait_ge(v_evac, NT * s + NT)
            if kt % 2 == 0:
                pe.wait_ge(exp_done, 40 * s + 2 * (GH * g + GH - 1) + kt // 2 + 3)
            for j in range(GH):
                h = GH * g + j
                ins = nc.tensor.matmul(ps[32 * j:32 * j + DH + 1, OB, :], v[:, kt, h, :], pr[:, h % RING, kt, :],
                                       start=(kt == 0), stop=(kt == NT - 1))
            if kt == NT - 1:
                ins.then_inc(o_ready, 1)

        def pe_mt(pe, s, g):
            pe.wait_ge(mh_ready, NG * s + g + 1)
            for qt in range(NT):
                ins = nc.tensor.matmul(ps[0:8, DB, qt * P:qt * P + P],
                                       mh[:, qt, :, :, :].rearrange("p r a h -> p (r a h)"), identb[:, :],
                                       start=True, stop=True)
            ins.then_inc(mt_ready, 1)

        def pe_op(pe, u, cross, what, bank=DB):
            base = ops_base(u, cross)
            if what == "t0":
                pe.wait_ge(xn_ready, NT * u + NT)
            if what == "c0":
                pe.wait_ge(cn_loaded, 32 * (u - B) + 32)
            if what in ("t0", "t1", "t2", "c0", "c1"):
                src, c = (xn if what[0] == "t" else cn), int(what[1])
                for t in range(NT):
                    toks = slice(t * P, t * P + P)
                    if what != "t2":
                        ins = nc.tensor.transpose(ps[:, bank, toks], src[:, t, c * P:c * P + P], ident[:, :])
                        continue
                    for half in (0, 64):
                        ins = nc.tensor.matmul(ps[half:half + 64, bank, toks], src[:, t, c * P:D], ident[:, :],
                                               start=True, stop=True)
            else:
                if what == QA:
                    pe.wait_ge(op_split, base + 3)
                    pe.wait_ge(raw_split, (SELF_CHUNKS if cross else 0) + QK_CHUNKS[cross])
                if what == KA and cross:
                    pe.wait_ge(op_split, op_value(u, cross, "c1"))
                todo = tile_products(what, cross)
                for n, (wt, d) in enumerate(todo):
                    ins = nc.tensor.matmul(ps[:, bank, :], wt, d, start=(n == 0), stop=(n == len(todo) - 1))
            ins.then_inc(op_ready, 1)

        def pe_v(pe, cross, t):
            if cross and t == 0:
                pe.wait_ge(raw_split, SELF_CHUNKS + CROSS_CHUNKS)
            todo = value_products(t, cross)
            for n, (d, wt) in enumerate(todo):
                ins = nc.tensor.matmul(ps[:, DB, 0:D], d, wt, start=(n == 0), stop=(n == len(todo) - 1))
            ins.then_inc(v_ready, 1)

        def pe_oproj(pe, s, cross, t, bank=DB):
            if t == 0:
                pe.wait_ge(norm_done, NG * s + NG)
                pe.wait_ge(wo_split, 3 if cross else 1)
            for g in range(NG):
                for wt in (wo1, wo2):
                    nc.tensor.matmul(ps[:, bank, 0:D], ons[:, g, t * P:t * P + P], wt[:, g, :],
                                     start=(g == 0 and wt is wo1), stop=False)
            ones = slice(MAX_ROW, MAX_ROW + 2)
            nc.tensor.matmul(ps[:, bank, 0:D], rows[ones, 2 * D:2 * D + P], rows[ones, cross * D:cross * D + D],
                             start=False, stop=True).then_inc(oproj_ready, 1)

        def op_value(u, cross, what):
            return ops_base(u, cross) + ops_of(cross).index(what) + 1

        def started(s, g):
            return isinstance(s, int) and s == 0 and g == 0

        def prologue_bank(k):
            return ST + k % 4

        def pe_slot(pe, s, cross, cross_next, prev, nxt, last):
            plan = dense_plan(cross_next)
            for g in range(NG):
                for j in range(GH):
                    tg, ts = (g + 2, s) if g + 2 < NG else (g + 2 - NG, s + 1)
                    smax = g + 2 < NG or nxt
                    pg, p_s = (g - 1, s) if g else (NG - 1, s - 1)
                    pv = j < 2 and (g > 0 or prev)
                    for half in range(2):
                        if smax:
                            pe_smax(pe, ts, tg, j, [2 * half])
                        if pv and j:
                            pe_pv(pe, p_s, pg, 2 * j + half)
                        if not started(s, g):
                            pe_st(pe, s, g, j, half)
                        if smax:
                            pe_smax(pe, ts, tg, j, [2 * half + 1])
                        if pv and not j:
                            pe_pv(pe, p_s, pg, 2 * j + half)
                        kind, what = plan.get(8 * g + 2 * j + half, (None, None))
                        if kind is None or not has(kind, what, g, prev, nxt):
                            continue
                        pe_free_wait(pe, last)
                        if kind == "mt":
                            mg, ms = (g + 1, s) if g + 1 < NG else (0, s + 1)
                            pe_mt(pe, ms, mg)
                            last = (mt_evac, NG * ms + mg + 1)
                        elif kind == "v":
                            pe_v(pe, cross, what)
                            last = (v_evac, NT * s + what + 1)
                        elif kind == "o":
                            pe_oproj(pe, s - 1, cross_prev(s, cross), what)
                            last = (res_done, NT * (s - 1) + what + 1)
                        else:
                            pe_op(pe, s + 1, cross_next, what)
                            last = (op_evac, op_value(s + 1, cross_next, what))

        def cross_prev(s, cross):
            return cross and not (isinstance(s, int) and s == B)

        def slots(emit):
            emit(0, False, False, False, True)
            yield range(1, B - 1), False
            emit(B - 1, False, True, True, True)
            emit(B, True, True, True, True)
            yield range(B + 1, UNITS - 1), True
            emit(UNITS - 1, True, True, True, False)

        def run_slots(eng, emit):
            for loop, cross in slots(emit):
                with eng.Fori(loop.start, loop.stop) as s:
                    emit(s, cross, cross, True, True)

        block = ctx.enter_context(nc.Block())

        @block.tensor
        def _(pe):
            pe.sem_inc(smax_free, 2)
            pe.sem_inc(exp_done, 2)
            pe.wait_ge(ident_ready, 2)
            for k, what in enumerate(OPS_SELF):
                if k >= 4:
                    pe.wait_ge(op_evac, k - 3)
                pe_op(pe, 0, False, what, prologue_bank(k))
            pe.wait_ge(ones_loaded, 48)
            pe.wait_ge(const_ready, 7)
            for j in range(GH):
                pe_smax(pe, 0, 0, j, range(NT))
            pe.wait_ge(op_evac, len(OPS_SELF))
            pe.wait_ge(raw_split, SELF_CHUNKS)
            pe.wait_ge(wo_split, 1)
            pe.wait_ge(bias_split, 1)
            pe_mt(pe, 0, 0)
            for j in range(GH):
                for half in range(2):
                    pe_smax(pe, 0, 1, j, (2 * half, 2 * half + 1))
                    pe_st(pe, 0, 0, j, half)

            def emit(s, cross, cross_next, prev, nxt):
                pe_slot(pe, s, cross, cross_next, prev, nxt, (mt_evac, NG * s + 1))
            run_slots(pe, emit)
            for kt in range(NT):
                pe_pv(pe, UNITS - 1, NG - 1, kt)
            for t in range(NT):
                pe_oproj(pe, UNITS - 1, True, t, ST + t)

        def act_exp(act, s, g, j, pair):
            h = GH * g + j
            act.wait_ge(st_ready, 40 * s + 2 * h + pair + 1)
            nc.scalar.activation(pr[:, h % RING, 2 * pair:2 * pair + 2, :], ps[:, ST + 2 * pair:ST + 2 * pair + 2, :],
                                 ACT.Exp, scale=SCALE).then_inc(exp_done, 1)

        def act_mt(act, s, g):
            act.wait_ge(mt_ready, NG * s + g + 1)
            act.wait_ge(max_placed, 16 * (NG * s + g))
            nc.scalar.activation(rows[0:8, 0:N], ps[0:8, DB, :], ACT.Copy).then_inc(mt_evac, 1)

        def act_o(act, s, g):
            act.wait_ge(o_ready, NG * s + g + 1)
            if g > 1 or not (isinstance(s, int) and s == 0):
                act.wait_ge(norm_done, NG * s + (0, -1, 1, 2, 3)[g])
            nc.scalar.activation(on[:, g % 2, :], ps[:, OB, :], ACT.Copy).then_inc(o_evac, 1)

        def act_round(act, s, g):
            act.wait_ge(scaled, NG * s + g + 1)
            if g == 0 and not (isinstance(s, int) and s == 0):
                act.wait_ge(oproj_ready, NT * s)
            nc.scalar.activation(ons[:, g, :], on[:, g % 2, :], ACT.Identity,
                                 scale=second[:, 1:2]).then_inc(norm_rounded, 1)

        def act_v(act, s, t):
            act.wait_ge(v_ready, NT * s + t + 1)
            nc.scalar.activation(v[:, t, :, 0:DH], ps[:, DB, 0:D].rearrange("p (h d) -> p h d", d=DH),
                                 ACT.Copy).then_inc(v_evac, 1)

        def act_op(act, u, cross, what, bank=DB):
            n = ops_base(u, cross) + ops_of(cross).index(what)
            norm = 1 if cross else 0
            act.wait_ge(op_ready, n + 1)
            k = ops_of(cross).index(what)
            if k >= 2 or not (isinstance(u, int) and u == 0):
                act.wait_ge(op_split, n - 1)
            if what in ("t0", "t1", "t2"):
                c = int(what[1])
                kw = dict(scale=gb[:, norm, c, 0:1], bias=gb[:, norm, c, 1:2])
                one, f = h1[:, c, :], ACT.Identity
            elif what in ("c0", "c1"):
                kw, one, f = {}, c1[:, int(what[1]), :], ACT.Copy
            else:
                kw, one, f = {}, sq[:, STAGE[what], 0, :], ACT.Copy
                before, sets = {QA: (1, u), KA: (1, u), QKC: (2, u), QB: (0, u + 1), KB: (0, u + 1)}[what]
                if not (isinstance(sets, int) and sets == 0):
                    act.wait_ge(stacked[before], STACK_DMAS * sets)
            nc.scalar.activation(one, ps[:, bank, :], f, **kw)
            nc.scalar.activation(whole[:, k % 2, :], ps[:, bank, :], f, **kw).then_inc(op_evac, 1)

        def act_slot(act, s, cross, cross_next, prev, nxt):
            plan = dense_plan(cross_next)
            for at in range(8 * NG):
                g, j, half = at // 8, at // 2 % GH, at % 2
                if not started(s, g):
                    act_exp(act, s, g, j, half)
                kind, what = plan.get(at, (None, None))
                if kind is not None and has(kind, what, g, prev, nxt):
                    if kind == "mt":
                        mg, ms = (g + 1, s) if g + 1 < NG else (0, s + 1)
                        act_mt(act, ms, mg)
                    elif kind == "v":
                        act_v(act, s, what)
                    elif kind == "op":
                        act_op(act, s + 1, cross_next, what)
                for after, step in ((ROUND, act_round), (EVAC, act_o)):
                    group = due(after, at, s, prev)
                    if group:
                        step(act, *group)
                if cross and not cross_prev(s, cross) and at == 26:
                    act_wo(act, True)
                if cross_next and not cross:
                    if at == 0:
                        act.wait_ge(w_zeroed, 4)
                    if at in WEIGHTS_AT:
                        act_weights(act, True, [WEIGHTS_AT.index(at)])

        @block.scalar
        def _(act):
            act_weights(act, False, range(2))
            act.wait_ge(small_loaded[0], 16 * 6)
            for k, what in enumerate(OPS_SELF):
                act_op(act, 0, False, what, prologue_bank(k))
                if k < 3:
                    act_weights(act, False, {0: (2, 3), 1: (4, 5), 2: (6, 7, 8)}[k])
            act.wait_ge(small_loaded[1], 16 * 6)
            act_wo(act, False)
            act.wait_ge(second_ready, 4)
            act.wait_ge(bias_loaded, 16 * 4)
            pair = slice(MAX_ROW, MAX_ROW + 2)
            nc.scalar.activation(rows[pair, 0:2 * D], flat_pr[pair, RAW_BIAS:RAW_BIAS + 2 * D], ACT.Identity,
                                 scale=second[pair, 3:4]).then_inc(bias_rounded, 1)
            act.wait_ge(mt_ready, 1)
            nc.scalar.activation(rows[0:8, 0:N], ps[0:8, DB, :], ACT.Copy).then_inc(mt_evac, 1)
            for j in range(GH):
                for pair in range(2):
                    act_exp(act, 0, 0, j, pair)

            def emit(s, cross, cross_next, prev, nxt):
                act_slot(act, s, cross, cross_next, prev, nxt)
            run_slots(act, emit)
            act_o(act, UNITS - 1, NG - 1)
            act_round(act, UNITS - 1, NG - 2)
            act_ff_weights(act, 0)
            act_ff_weights(act, 1)
            act_round(act, UNITS - 1, NG - 1)
            act_ff_weights(act, 2)
            act_ff_weights(act, 3)

        def dve_smax(dve, s, g, j, qt):
            h = GH * g + j
            if j == 0 and qt == 0:
                dve.wait_ge(mh_ready, NG * s + g)
            dve.wait_ge(smax_ready, 80 * s + 4 * h + qt + 1)
            nc.vector.tensor_reduce(nm[:, qt, j % 2, j // 2:j // 2 + 1], ps[:, SM + qt % 2, :], AX_X, ALU.max,
                                    negate=True).then_inc(smax_free, 1)

        def dve_parts(dve, s, g):
            dve.wait_ge(smax_free, 80 * s + 16 * g + 18)
            if not (isinstance(s, int) and s == 0 and g == 0):
                dve.wait_ge(mt_ready, NG * s + g)
            nc.vector.tensor_copy(mh[:, :, :, 0, :], nm[:, :, :, :]).then_inc(mh_high, 1)
            dve.wait_ge(mh_high, NG * s + g + 1)
            nc.vector.tensor_tensor(mh[:, :, :, 1, :], nm[:, :, :, :], mh[:, :, :, 0, :],
                                    ALU.subtract).then_inc(mh_ready, 1)

        def dve_stats(dve, u, t):
            if t == 0:
                dve.wait_ge(xl_loaded, 16 * u + 16)
            nc.vector.bn_stats(mv6[:, t, :], xn[:, t, 0:D]).then_inc(stats_raw, 1)

        def dve_stats_end(dve, u):
            if not (isinstance(u, int) and u == 0):
                wait_apart(dve, nmr_ready, u, const_ready)
            wait_apart(dve, stats_raw, NT * u + NT, const_ready)
            for t in range(NT):
                nc.vector.bn_aggr(mv[:, t, :], mv6[:, t, :]).then_inc(stats_mv, 1)
            dve.wait_ge(stats_mv, NT * u + NT)
            nc.vector.tensor_scalar(negmean[:, :], mv[:, :, 0], -1.0, None, ALU.mult).then_inc(stats_ready, 1)
            nc.vector.tensor_scalar(vareps[:, :], mv[:, :, 1], EPS, None, ALU.add).then_inc(stats_ready, 1)

        def dve_res(dve, s, t, bank=DB):
            if t == 0:
                dve.wait_ge(xr_loaded, 16 * s + 16)
            dve.wait_ge(oproj_ready, NT * s + t + 1)
            nc.vector.tensor_tensor(xr[:, t, :], ps[:, bank, 0:D], xr[:, t, :], ALU.add).then_inc(res_done, 1)

        def dve_inv(dve, s, g):
            dve.wait_ge(sums_spread, 16 * (NG * s + g) + 16)
            if not (isinstance(s, int) and s == 0 and g == 0):
                dve.wait_ge(inv_placed, 16 * (NG * s + g))
            nc.vector.reciprocal(inv[:, :], sums[:, :]).then_inc(inv_ready, 1)

        def dve_spread(dve, s, g):
            wait_apart(dve, inv_placed, 16 * (NG * s + g) + 16, const_ready)
            nc.vector.stream_shuffle(rs[:, :], rs[:, :], [DH] * 32).then_inc(rs_ready, 1)
            nc.vector.stream_shuffle(on[:, g % 2, :], on[:, g % 2, :], list(range(DH)) * 2).then_inc(rs_ready, 1)

        def dve_rest(dve, s, g):
            dve.wait_ge(norm_rounded, NG * s + g + 1)
            nc.vector.scalar_tensor_tensor(out=ons[:, g, :], in0=on[:, g % 2, :], scalar=second[:, 0:1],
                                           in1=ons[:, g, :], op0=ALU.mult, op1=ALU.add).then_inc(norm_done, 1)

        def dve_slot(dve, s, cross, cross_next, prev, nxt):
            for at in range(8 * NG):
                g, j, half = at // 8, at // 2 % GH, at % 2
                tg, ts = (g + 2, s) if g + 2 < NG else (g + 2 - NG, s + 1)
                smax = g + 2 < NG or nxt
                if smax:
                    for qt in (2 * half, 2 * half + 1):
                        dve_smax(dve, ts, tg, j, qt)
                    if at % 8 == 7:
                        dve_parts(dve, ts, tg)
                if at in (2, 3) and nxt:
                    for t in (2 * at - 4, 2 * at - 3):
                        dve_stats(dve, s + 1, t)
                if at == 4 and nxt:
                    dve_stats_end(dve, s + 1)
                for after, step in ((REST, dve_rest), (INV, dve_inv), (SPREAD, dve_spread)):
                    group = due(after, at, s, prev)
                    if group:
                        step(dve, *group)
                if cross and not cross_prev(s, cross) and at == 28:
                    dve_wo(dve, True)
                if 12 <= at < 12 + NT and prev:
                    dve_res(dve, s - 1, at - 12)

        @block.vector
        def _(dve):
            nc.vector.memset(v[:, :, :, DH:DH + 1], 1.0).then_inc(const_ready, 1)
            nc.vector.memset(ps[:, OB, :], 0.0).then_inc(const_ready, 1)
            nc.vector.memset(rs[:, :], 0.0).then_inc(const_ready, 1)
            for t in range(NT):
                dve_stats(dve, 0, t)
            dve_stats_end(dve, 0)
            split_weights(dve, nc.vector, False, range(SELF_CHUNKS))
            nc.vector.memset(ks[:, H // 2:H, :].bitcast(F32), 0.0).then_inc(const_ready, 1)
            dve.wait_ge(ident_ready, 2)
            nc.vector.tensor_reduce(second[:, 2:3], ident[:, 1:P:32], AX_X, ALU.add).then_inc(second_ready, 1)
            wait_apart(dve, second_ready, 1, const_ready)
            nc.vector.stream_shuffle(second[:, 0:1], second[:, 2:3], [0] * DH + [1] * DH).then_inc(second_ready, 1)
            dve.wait_ge(second_ready, 2)
            for k in (0, 2):
                nc.vector.tensor_scalar(second[:, k + 1:k + 2], second[:, k:k + 1], -2.0, 1.0,
                                        ALU.mult, ALU.add).then_inc(second_ready, 1)
            dve_wo(dve, False)
            dve.wait_ge(bias_rounded, 1)
            pair = slice(MAX_ROW, MAX_ROW + 2)
            nc.vector.scalar_tensor_tensor(out=rows[pair, 0:2 * D], in0=flat_pr[pair, RAW_BIAS:RAW_BIAS + 2 * D],
                                           scalar=second[pair, 2:3], in1=rows[pair, 0:2 * D], op0=ALU.mult,
                                           op1=ALU.add).then_inc(bias_split, 1)
            for g in (0, 1):
                for j in range(GH):
                    for qt in range(NT):
                        dve_smax(dve, 0, g, j, qt)
                dve_parts(dve, 0, g)

            def emit(s, cross, cross_next, prev, nxt):
                dve_slot(dve, s, cross, cross_next, prev, nxt)
            run_slots(dve, emit)
            dve_inv(dve, UNITS - 1, NG - 2)
            dve_spread(dve, UNITS - 1, NG - 2)
            dve_inv(dve, UNITS - 1, NG - 1)
            dve_rest(dve, UNITS - 1, NG - 2)
            dve_spread(dve, UNITS - 1, NG - 1)
            split_ff_weights(dve, nc.vector, 0)
            dve_rest(dve, UNITS - 1, NG - 1)
            split_ff_weights(dve, nc.vector, 1)
            for t in range(NT):
                dve_res(dve, UNITS - 1, t, ST + t)
            split_ff_weights(dve, nc.vector, 2)

        def pool_norm(pool, u, cross):
            pool.wait_ge(stats_ready, 2 * u + 2)
            nc.gpsimd.tensor_tensor(rstd[:, :], vareps[:, :], neghalf[:, :], ALU.pow).then_inc(rstd_ready, 1)
            pool.wait_ge(rstd_ready, u + 1)
            nc.gpsimd.tensor_tensor(nmr[:, :], negmean[:, :], rstd[:, :], ALU.mult).then_inc(nmr_ready, 1)
            wait_apart(pool, nmr_ready, u + 1, ident_ready)
            for t in range(NT):
                nc.gpsimd.tensor_scalar(xn[:, t, :], xn[:, t, :], rstd[:, t:t + 1], nmr[:, t:t + 1],
                                        ALU.mult, ALU.add).then_inc(xn_ready, 1)

        def pool_split(pool, u, cross, what):
            n = ops_base(u, cross) + ops_of(cross).index(what)
            k = ops_of(cross).index(what)
            pool.wait_ge(op_evac, n + 1)
            if what in ("t2", "c1") or k and ops_of(cross)[k - 1] in ("t2", "c1"):
                pool.wait_ge(op_split, n)
            a = slice(64, P) if what in ("t2", "c1") else slice(0, P)
            one, two = {
                "t0": (h1[:, 0, :], h2[:, 0, :]), "t1": (h1[:, 1, :], h2[:, 1, :]), "t2": (h1[a, 2, :], h1[a, 2, :]),
                "c0": (c1[:, 0, :], c2[:, :]), "c1": (c1[a, 1, :], c1[a, 1, :]),
            }.get(what) or (sq[:, STAGE[what], 0, :], sq[:, STAGE[what], 1, :])
            nc.gpsimd.tensor_tensor(two, whole[a, k % 2, :], one, ALU.subtract).then_inc(op_split, 1)

        def pool_scale(pool, s, g):
            pool.wait_ge(rs_ready, 2 * (NG * s + g) + 2)
            nc.gpsimd.tensor_tensor(on[:, g % 2, :], on[:, g % 2, :], rs[:, :], ALU.mult).then_inc(scaled, 1)

        def pool_slot(pool, s, cross, cross_next, prev, nxt):
            to_cross = cross_next and not cross

            def weights(chunks):
                if to_cross:
                    split_weights(pool, nc.gpsimd, True, chunks)

            def splits(names):
                if nxt:
                    for what in names:
                        pool_split(pool, s + 1, cross_next, what)

            if to_cross:
                pool_zero_halves(pool)
            weights(range(4))
            if prev:
                pool_scale(pool, s - 1, NG - 2)
            if nxt:
                pool_norm(pool, s + 1, cross_next)
            if prev:
                pool_scale(pool, s - 1, NG - 1)
            splits(ops_of(cross_next)[:3])
            if to_cross:
                pool.wait_ge(op_split, op_value(s + 1, True, "t2"))
            weights([4])
            splits(ops_of(cross_next)[3:4])
            weights([5])
            splits(ops_of(cross_next)[4:-2])
            pool_scale(pool, s, 0)
            weights([6])
            splits([QB])
            pool_scale(pool, s, 1)
            splits([KB])
            pool_scale(pool, s, 2)

        @block.gpsimd
        def _(pool):
            nc.gpsimd.memset(ident[:, :], 0.0).then_inc(ident_zero, 1)
            nc.gpsimd.memset(identb[:, :], 0.0).then_inc(ident_zero, 1)
            nc.gpsimd.memset(neghalf[:, :], -0.5).then_inc(ident_zero, 1)
            pool.wait_ge(ident_zero, 3)
            for m in (ident, identb):
                nc.gpsimd.affine_select(out=m[:, :], in_=m[:, :], compare_op=ALU.not_equal, fill=1.0, base=0,
                                        pattern=[[-1, P]], channel_multiplier=1).then_inc(ident_ready, 1)
            nc.gpsimd.memset(qs[:, :, :].bitcast(F32), 0.0).then_inc(const_ready, 1)
            pool_norm(pool, 0, False)
            for what in OPS_SELF[:3]:
                pool_split(pool, 0, False, what)
            pool.wait_ge(op_split, 3)
            nc.gpsimd.memset(ks[:, 0:H // 2, :].bitcast(F32), 0.0).then_inc(const_ready, 1)
            nc.gpsimd.memset(flat_pr[0:2, 0:ONES], 1.0).then_inc(const_ready, 1)
            for what in OPS_SELF[3:]:
                pool_split(pool, 0, False, what)

            def emit(s, cross, cross_next, prev, nxt):
                pool_slot(pool, s, cross, cross_next, prev, nxt)
            run_slots(pool, emit)
            for g in (NG - 2, NG - 1):
                pool_scale(pool, UNITS - 1, g)
            split_ff_weights(pool, nc.gpsimd, 3)

        def tokens(t, b):
            return t[b].rearrange("(t p) d -> p t d", p=P)

        def sp_stack(sp, u, cross, which, side):
            tile = {0: (QA, KA), 1: (QB, KB), 2: (QKC, QKC)}[which][side]
            pair0, pairs = ((0, 4), (4, 4), (8, 2))[which]
            sp.wait_ge(op_split, op_value(u, cross, tile))
            n = 64 if which < 2 else 32
            first = 64 * side if which == 2 else 0
            for row, *parts in STACK:
                src = sq[:, STAGE[tile], parts[side], :].bitcast(F32)
                if side == 0:
                    sp.dma_start(qs[2 * DH * row:2 * DH * (row + 1), pair0:pair0 + pairs, :].bitcast(F32),
                                 src[first:first + 2 * n, :]).then_inc(stacked[which], 16)
                    continue
                for par in range(2):
                    rows = slice(DH * (2 * row + par), DH * (2 * row + par + 1))
                    sp.dma_start(ks[rows, 2 * pair0 + par:2 * (pair0 + pairs):2, :].bitcast(F32),
                                 src[first + par * n:first + par * n + n, :]).then_inc(stacked[which], 16)

        def sp_max(sp, s, g):
            sp.wait_ge(mt_evac, NG * s + g + 1)
            sp.dma_start(qs[MAX_ROW:MAX_ROW + 4, 2 * g:2 * g + 2, :].bitcast(F32),
                         rows[0:8, 0:N].bitcast(F32)).then_inc(max_placed, 16)

        def sp_sums(sp, s, g):
            wait_apart(sp, o_evac, NG * s + g + 1, ident_zero)
            if not (isinstance(s, int) and s == 0 and g == 0):
                sp.wait_ge(inv_ready, NG * s + g)
            sp.dma_start(sums[:, :], on[DH:P:32, g % 2, :]).then_inc(sums_spread, 16)

        def sp_inv(sp, s, g):
            if not (isinstance(s, int) and s == 0 and g == 0):
                wait_apart(sp, scaled, NG * s + g, ident_zero)
            sp.wait_ge(inv_ready, NG * s + g + 1)
            sp.dma_start(rs[DH:P:32, :], inv[:, :]).then_inc(inv_placed, 16)

        def sp_context(sp, b):
            sp.dma_start(cn[:, :, 0:C], tokens(ctx_in, b)).then_inc(cn_loaded, 16)
            sp.dma_start(cn[:, :, C:2 * P], tokens(ctx_in, b)[:, :, P:C]).then_inc(cn_loaded, 16)

        def sp_slot(sp, s, cross, cross_next, prev, nxt):
            src = x1 if cross_prev(s, cross) else x
            dst = x2 if cross_prev(s, cross) else x1
            if cross_next and not cross:
                sp_weights(sp, True, range(4))
            if nxt:
                sp.wait_ge(op_ready, ops_base(s, cross) + 3)
                if cross_next:
                    sp.wait_ge(x_stored, 16 * (s - (B - 2)))
                    sp.dma_start(xn[:, :, :], tokens(x1, s - (B - 1))).then_inc(xl_loaded, 16)
                    if cross:
                        sp.wait_ge(op_ready, op_value(s, True, "c1"))
                        sp_context(sp, s - (B - 1))
                else:
                    sp.dma_start(xn[:, :, :], tokens(x, s + 1)).then_inc(xl_loaded, 16)
            if prev:
                if not (isinstance(s, int) and s == 1):
                    sp.wait_ge(x_stored, 16 * (s - 1))
                if cross_prev(s, cross):
                    sp.wait_ge(wo_split, 3)
                b = s - 1 - (B if cross_prev(s, cross) else 0)
                sp.dma_start(xr[:, :, :], tokens(src, b)).then_inc(xr_loaded, 16)
            if prev:
                sp_inv(sp, s - 1, NG - 2)
            sp_max(sp, s, 1)
            if prev:
                sp_sums(sp, s - 1, NG - 1)
                wait_apart(sp, st_ready, 40 * s, ident_zero)
            sp_stack(sp, s, cross, 2, 0)
            if prev:
                sp_inv(sp, s - 1, NG - 1)
            sp_stack(sp, s, cross, 2, 1)
            if cross_next and not cross:
                sp_weights(sp, True, [4])
                sp_context(sp, 0)
            sp_max(sp, s, 2)
            if not nxt:
                sp_ff_weights(sp, 0)
            if prev:
                sp.wait_ge(res_done, NT * s)
                sp.dma_start(tokens(dst, b), xr[:, :, :]).then_inc(x_stored, 16)
            if isinstance(s, int) and s == B:
                sp.wait_ge(oproj_ready, NT * B)
                sp.wait_ge(x_stored, 16 * B)
                sp_wo(sp, True)
            if cross_next and not cross:
                sp.wait_ge(v_ready, NT * B)
                sp_weights(sp, True, [5])
            sp_sums(sp, s, 0)
            if nxt:
                wait_apart(sp, st_ready, 40 * s + 16, ident_zero)
                sp_stack(sp, s + 1, cross_next, 0, 0)
            sp_inv(sp, s, 0)
            if nxt:
                sp_stack(sp, s + 1, cross_next, 0, 1)
            sp_max(sp, s, 3)
            if cross_next and not cross:
                sp_weights(sp, True, [6])
            if not nxt:
                sp_ff_weights(sp, 1)
            sp_sums(sp, s, 1)
            sp_inv(sp, s, 1)
            if not nxt:
                sp_ff_weights(sp, 2)
            sp_max(sp, s, 4)
            if not nxt:
                sp_ff_weights(sp, 3)
            sp_sums(sp, s, 2)
            sp_inv(sp, s, 2)
            if nxt:
                wait_apart(sp, st_ready, 40 * s + 32, ident_zero)
                sp_stack(sp, s + 1, cross_next, 1, 0)
                sp_max(sp, s + 1, 0)
            if nxt:
                sp_stack(sp, s + 1, cross_next, 1, 1)
            sp_sums(sp, s, 3)

        @block.sync
        def _(sp):
            sp.dma_start(xn[:, :, :], tokens(x, 0)).then_inc(xl_loaded, 16)
            sp_weights(sp, False, range(2))
            for k, name in enumerate(("n1", "n2")):
                for q, part in enumerate(("_g", "_b")):
                    vec = w[name + part].rearrange("(p a) -> p a", a=1)
                    sp.dma_start(gb[:, k, 0:2, q], w[name + part][0:2 * P].rearrange("(c p) -> p c", p=P),
                                 allow_slow_non_contiguous=True).then_inc(small_loaded[k], 16)
                    sp.dma_start(gb[0:64, k, 2, q:q + 1], vec[2 * P:D]).then_inc(small_loaded[k], 16)
                    sp.dma_start(gb[64:P, k, 2, q:q + 1], vec[2 * P:D]).then_inc(small_loaded[k], 16)
                if k == 0:
                    sp_weights(sp, False, range(2, SELF_CHUNKS))
            sp_wo(sp, False)
            for part in range(2):
                for k, name in enumerate(("o1_b", "o2_b")):
                    sp.dma_start(flat_pr[MAX_ROW + part:MAX_ROW + part + 1, RAW_BIAS + k * D:RAW_BIAS + k * D + D],
                                 w[name].rearrange("(a n) -> a n", a=1)).then_inc(bias_loaded, 16)
            sp.wait_ge(const_ready, 7)
            ones = flat_pr[0:2, 0:ONES]
            for par in range(2):
                first = MAX_ROW + 2 * par
                sp.dma_start(ks[first:first + 2, par:H:2, :].bitcast(F32),
                             ones.rearrange("p (h n) -> p h n", n=N)).then_inc(ones_loaded, 16)
            sp.dma_start(rows[MAX_ROW:MAX_ROW + 2, 2 * D:2 * D + P].bitcast(F32), ones[:, 0:P]).then_inc(ones_loaded, 16)
            for which in (0, 1):
                for side in (0, 1):
                    sp_stack(sp, 0, False, which, side)
            sp_max(sp, 0, 0)

            def emit(s, cross, cross_next, prev, nxt):
                sp_slot(sp, s, cross, cross_next, prev, nxt)
            run_slots(sp, emit)
            u = UNITS - 1
            sp_inv(sp, u, NG - 2)
            sp_sums(sp, u, NG - 1)
            sp_inv(sp, u, NG - 1)
            sp.wait_ge(x_stored, 16 * u)
            sp.dma_start(xr[:, :, :], tokens(x1, B - 1)).then_inc(xr_loaded, 16)
            sp.wait_ge(res_done, NT * UNITS)
            sp.dma_start(tokens(x2, B - 1), xr[:, :, :]).then_inc(x_stored, 16)
            sp.wait_ge(x_stored, 16 * UNITS)
    return wa1, wa2, wb1, wb2


def feed_forward(nc, x2, w, weights, out):
    with ExitStack() as ctx:
        def sb(name, shape, dt=F32):
            return ctx.enter_context(nc.sbuf_tensor("ff_" + name, shape, dt))

        def sem(name):
            return ctx.enter_context(nc.semaphore("ff_" + name))

        ps = ctx.enter_context(nc.psum_tensor("ff_ps", [P, 8, 512], F32))
        ACC, AG, TB = 0, 4, 7

        def token_bank(b, c):
            return ACC + c if isinstance(b, int) and b == 0 else TB

        def gate_bank(f):
            return AG + 2 * f % 3

        def value_bank(f):
            return AG + (2 * f + 1) % 3

        xl = sb("xl", [P, NT, D])
        xr = sb("xr", [P, NT, D])
        y = sb("y", [P, NT, D])
        xn = sb("xn", [P, NT, 3 * P])
        mv6 = sb("mv6", [P, NT, 6])
        mv = sb("mv", [P, NT, 2])
        negmean = sb("negmean", [P, NT])
        vareps = sb("vareps", [P, NT])
        rstd = sb("rstd", [P, NT])
        nmr = sb("nmr", [P, NT])
        neghalf = sb("neghalf", [P, NT])
        gb = sb("gb", [P, 3, 2])
        b1 = sb("b1", [P, 2 * MC])
        b2 = sb("b2", [P, D])
        h1 = sb("h1", [P, 2, 3, N], F32R)
        h2 = sb("h2", [P, 2, 2, N], F32R)
        whole = sb("whole", [P, 3, N])
        gate = sb("gate", [P, 2, N])
        u = sb("u", [P, 3, N])
        u1 = sb("u1", [P, 3, N], F32R)
        u2 = sb("u2", [P, 3, N], F32R)
        wa1, wa2, wb1, wb2 = weights
        ident = sb("ident", [P, P])

        ident_zero = sem("ident_zero")
        ident_ready = sem("ident_ready")
        small_loaded = sem("small_loaded")
        xl_loaded = sem("xl_loaded")
        xr_loaded = sem("xr_loaded")
        y_stored = sem("y_stored")
        stats_raw = sem("stats_raw")
        stats_mv = sem("stats_mv")
        stats_ready = sem("stats_ready")
        rstd_ready = sem("rstd_ready")
        nmr_ready = sem("nmr_ready")
        xn_ready = sem("xn_ready")
        t_ready = sem("t_ready")
        t_evac = sem("t_evac")
        t_split = sem("t_split")
        ag_ready = sem("ag_ready")
        gate_ready = sem("gate_ready")
        u_ready = sem("u_ready")
        u1_ready = sem("u1_ready")
        u2_ready = sem("u2_ready")
        acc_ready = sem("acc_ready")
        y_ready = sem("y_ready")
        b2_added = sem("b2_added")

        def each_batch(eng, emit):
            emit(0, True, 0)
            with eng.Fori(1, B // 2) as i:
                emit(2 * i - 1, True, 1)
                emit(2 * i, True, 0)
            emit(B - 1, False, 1)

        FEATURES_AT = 5

        block = ctx.enter_context(nc.Block())

        def tokens(t, b):
            return t[b].rearrange("(t p) d -> p t d", p=P)

        @block.sync
        def _(sp):
            sp.dma_start(xl[:, :, :], tokens(x2, 0)).then_inc(xl_loaded, 16)
            for q, part in enumerate(("n3_g", "n3_b")):
                vec = w[part].rearrange("(p a) -> p a", a=1)
                sp.dma_start(gb[:, 0, q:q + 1], vec[0:P]).then_inc(small_loaded, 16)
                sp.dma_start(gb[:, 1, q:q + 1], vec[P:2 * P]).then_inc(small_loaded, 16)
                sp.dma_start(gb[0:64, 2, q:q + 1], vec[2 * P:D]).then_inc(small_loaded, 16)
                sp.dma_start(gb[64:P, 2, q:q + 1], vec[2 * P:D]).then_inc(small_loaded, 16)
            sp.dma_start(b1[:, :], w["ff_b1"].rearrange("(c p) -> p c", p=P),
                         allow_slow_non_contiguous=True).then_inc(small_loaded, 16)
            sp.dma_start(b2[:, :], w["ff_b2"].rearrange("(a n) -> a n", a=1).broadcast_to([P, D]))\
              .then_inc(small_loaded, 16)

            def emit(b, nxt, par):
                if nxt:
                    sp.wait_ge(xn_ready, 2 * NT * b + 2 * NT)
                    sp.dma_start(xl[:, :, :], tokens(x2, b + 1)).then_inc(xl_loaded, 16)
                sp.wait_ge(y_ready, NT * b)
                sp.dma_start(xr[:, :, :], tokens(x2, b)).then_inc(xr_loaded, 16)
                sp.wait_ge(y_ready, NT * b + NT)
                sp.dma_start(tokens(out, b), y[:, :, :]).then_inc(y_stored, 16)
            each_batch(sp, emit)
            sp.wait_ge(y_stored, 16 * B)

        @block.tensor
        def _(pe):
            def transposes(b, c):
                if c == 0:
                    pe.wait_ge(xn_ready, 2 * NT * b + 2 * NT)
                if not (isinstance(b, int) and b == 0):
                    pe.wait_ge(t_evac, 3 * b + c)
                for t in range(NT):
                    ins = nc.tensor.transpose(ps[:, token_bank(b, c), t * P:t * P + P], xn[:, t, c * P:c * P + P], ident[:, :])
                ins.then_inc(t_ready, 1)

            def pair(b, f, par):
                if f == 0:
                    pe.wait_ge(t_split, 3 * b + 3)
                for side in (1, 0):
                    if side and f:
                        pe.wait_ge(u_ready, MC * b + f - 1)
                    elif side or f:
                        pe.wait_ge(gate_ready, MC * b + (0 if side else f))
                    else:
                        pe.wait_ge(u_ready, MC * b)
                    cols = slice(side * F + f * P, side * F + f * P + P)
                    todo = ([(wa1[:, c, cols], h1[:, par, c, :]) for c in range(3)]
                            + [(wa2[:, c, cols], h1[:, par, c, :]) for c in range(2)]
                            + [(wa2[0:64, 2, cols], h1[0:64, par, 2, :])]
                            + [(wa1[:, c, cols], h2[:, par, c, :]) for c in range(2)])
                    for n, (wt, d) in enumerate(todo):
                        ins = nc.tensor.matmul(ps[:, gate_bank(f) if side else value_bank(f), :], wt, d,
                                               start=(n == 0), stop=(n == len(todo) - 1))
                    ins.then_inc(ag_ready, 1)

            def down(b, f):
                if f == 0:
                    pe.wait_ge(y_ready, NT * b)
                pe.wait_ge(u1_ready, MC * b + f + 1)
                for t in range(NT):
                    toks = slice(t * P, t * P + P)
                    nc.tensor.matmul(ps[:, ACC + t, 0:D], u1[:, f % 3, toks], wb1[:, f, :], start=(f == 0), stop=False)
                    ins = nc.tensor.matmul(ps[:, ACC + t, 0:D], u1[:, f % 3, toks], wb2[:, f, :], start=False, stop=False)
                pe.wait_ge(u2_ready, MC * b + f + 1)
                for t in range(NT):
                    toks = slice(t * P, t * P + P)
                    ins = nc.tensor.matmul(ps[:, ACC + t, 0:D], u2[:, f % 3, toks], wb1[:, f, :],
                                           start=False, stop=(f == MC - 1))
                    if f == MC - 1:
                        ins.then_inc(acc_ready, 1)

            pe.wait_ge(ident_ready, 1)
            for c in range(3):
                transposes(0, c)

            def emit(b, nxt, par):
                for f in range(MC):
                    pair(b, f, par)
                    if f >= 2:
                        down(b, f - 2)
                    if nxt and FEATURES_AT <= f < FEATURES_AT + 3:
                        transposes(b + 1, f - FEATURES_AT)
                down(b, MC - 2)
                down(b, MC - 1)
            each_batch(pe, emit)

        @block.scalar
        def _(act):
            def features(b, par, c):
                act.wait_ge(t_ready, 3 * b + c + 1)
                if c == 0 and not (isinstance(b, int) and b == 0):
                    act.wait_ge(t_split, 3 * b)
                kw = dict(scale=gb[:, c, 0:1], bias=gb[:, c, 1:2])
                nc.scalar.activation(h1[:, par, c, :], ps[:, token_bank(b, c), :], ACT.Identity, **kw)
                nc.scalar.activation(whole[:, c, :], ps[:, token_bank(b, c), :], ACT.Identity, **kw).then_inc(t_evac, 1)

            act.wait_ge(small_loaded, 16 * 10)
            for c in range(3):
                features(0, 0, c)

            def rounded(b, f):
                act.wait_ge(u_ready, MC * b + f + 1)
                nc.scalar.activation(u1[:, f % 3, :], u[:, f % 3, :], ACT.Copy).then_inc(u1_ready, 1)

            def emit(b, nxt, par):
                for f in range(MC):
                    act.wait_ge(ag_ready, 2 * MC * b + 2 * f + 1)
                    if f < 2:
                        act.wait_ge(u_ready, MC * b)
                    nc.scalar.activation(gate[:, f % 2, :], ps[:, gate_bank(f), :], ACT.Gelu,
                                         bias=b1[:, MC + f:MC + f + 1]).then_inc(gate_ready, 1)
                    if f:
                        rounded(b, f - 1)
                    if nxt and FEATURES_AT <= f < FEATURES_AT + 3:
                        features(b + 1, 1 - par, f - FEATURES_AT)
                rounded(b, MC - 1)
            each_batch(act, emit)

        @block.vector
        def _(dve):
            def stats(b):
                dve.wait_ge(xl_loaded, 16 * b + 16)
                for t in range(NT):
                    nc.vector.bn_stats(mv6[:, t, :], xl[:, t, :]).then_inc(stats_raw, 1)
                wait_apart(dve, nmr_ready, b, xl_loaded)
                wait_apart(dve, stats_raw, NT * b + NT, xl_loaded)
                for t in range(NT):
                    nc.vector.bn_aggr(mv[:, t, :], mv6[:, t, :]).then_inc(stats_mv, 1)
                dve.wait_ge(stats_mv, NT * b + NT)
                nc.vector.tensor_scalar(negmean[:, :], mv[:, :, 0], -1.0, None, ALU.mult).then_inc(stats_ready, 1)
                nc.vector.tensor_scalar(vareps[:, :], mv[:, :, 1], EPS, None, ALU.add).then_inc(stats_ready, 1)

            stats(0)

            def emit(b, nxt, par):
                for f in range(MC):
                    dve.wait_ge(ag_ready, 2 * MC * b + 2 * f + 2)
                    dve.wait_ge(gate_ready, MC * b + f + 1)
                    if f < 3:
                        dve.wait_ge(u2_ready, MC * b)
                    else:
                        dve.wait_ge(u2_ready, MC * b + f - 2)
                    nc.vector.scalar_tensor_tensor(out=u[:, f % 3, :], in0=ps[:, value_bank(f), :],
                                                   scalar=b1[:, f:f + 1], in1=gate[:, f % 2, :],
                                                   op0=ALU.add, op1=ALU.mult).then_inc(u_ready, 1)
                    if f == 1 and nxt:
                        stats(b + 1)
                dve.wait_ge(b2_added, NT * b + NT)
                dve.wait_ge(y_stored, 16 * b)
                for t in range(NT):
                    dve.wait_ge(acc_ready, NT * b + t + 1)
                    nc.vector.tensor_tensor(y[:, t, :], ps[:, ACC + t, 0:D], xr[:, t, :], ALU.add).then_inc(y_ready, 1)
            each_batch(dve, emit)

        @block.gpsimd
        def _(pool):
            nc.gpsimd.memset(ident[:, :], 0.0).then_inc(ident_zero, 1)
            nc.gpsimd.memset(neghalf[:, :], -0.5).then_inc(ident_zero, 1)
            pool.wait_ge(ident_zero, 2)
            nc.gpsimd.affine_select(out=ident[:, :], in_=ident[:, :], compare_op=ALU.not_equal, fill=1.0, base=0,
                                    pattern=[[-1, P]], channel_multiplier=1).then_inc(ident_ready, 1)

            def norm(b):
                pool.wait_ge(stats_ready, 2 * b + 2)
                nc.gpsimd.tensor_tensor(rstd[:, :], vareps[:, :], neghalf[:, :], ALU.pow).then_inc(rstd_ready, 1)
                pool.wait_ge(rstd_ready, b + 1)
                nc.gpsimd.tensor_tensor(nmr[:, :], negmean[:, :], rstd[:, :], ALU.mult).then_inc(nmr_ready, 1)
                wait_apart(pool, nmr_ready, b + 1, ident_ready)
                wait_apart(pool, t_ready, 3 * b, ident_ready)
                for t in range(NT):
                    for a, e in ((0, D), (2 * P, D)):
                        to = a if a == 0 else D
                        nc.gpsimd.tensor_scalar(xn[:, t, to:to + e - a], xl[:, t, a:e], rstd[:, t:t + 1],
                                                nmr[:, t:t + 1], ALU.mult, ALU.add).then_inc(xn_ready, 1)

            def features(b, par, c):
                pool.wait_ge(t_evac, 3 * b + c + 1)
                a = slice(64, P) if c == 2 else slice(0, P)
                two = h1[a, par, 2, :] if c == 2 else h2[:, par, c, :]
                nc.gpsimd.tensor_tensor(two, whole[a, c, :], h1[a, par, c, :], ALU.subtract).then_inc(t_split, 1)
                if c:
                    pool.wait_ge(t_split, 3 * b + c + 1)

            norm(0)
            for c in range(3):
                features(0, 0, c)
            pool.wait_ge(small_loaded, 16 * 10)

            def emit(b, nxt, par):
                for f in range(MC):
                    pool.wait_ge(u1_ready, MC * b + f + 1)
                    nc.gpsimd.tensor_tensor(u2[:, f % 3, :], u[:, f % 3, :], u1[:, f % 3, :],
                                            ALU.subtract).then_inc(u2_ready, 1)
                    if f == 2 and nxt:
                        norm(b + 1)
                    if f == 4:
                        pool.wait_ge(xr_loaded, 16 * b + 16)
                        for t in range(NT):
                            nc.gpsimd.tensor_tensor(xr[:, t, :], xr[:, t, :], b2[:, :], ALU.add).then_inc(b2_added, 1)
                    if nxt and f == FEATURES_AT + 2:
                        pool.wait_ge(u2_ready, MC * b + f + 1)
                    if nxt and FEATURES_AT <= f < FEATURES_AT + 3:
                        features(b + 1, 1 - par, f - FEATURES_AT)
            each_batch(pool, emit)


def layer(nc, x, ctx_in, w, out):
    x1 = nc.dram_tensor("x_after_self", [B, N, D], F32).ap()
    x2 = nc.dram_tensor("x_after_cross", [B, N, D], F32).ap()
    with ExitStack() as outer:
        weights = attention(nc, x, ctx_in, w, x1, x2, outer)
        feed_forward(nc, x2, w, weights, out)


_WEIGHTS = ["n1_g", "n1_b", "q1", "k1", "v1", "o1_w", "o1_b", "n2_g", "n2_b", "q2", "k2", "v2", "o2_w", "o2_b",
            "n3_g", "n3_b", "ff_w1", "ff_b1", "ff_w2", "ff_b2"]


def kernel(**inputs):
    import numpy as _np
    import concourse.bacc as _bacc
    from concourse import mybir as _mybir
    from concourse.bass_utils import run_bass_kernel_spmd as _run

    nc = _bacc.Bacc("TRN2", target_bir_lowering=False, num_devices=1)
    arrays, aps = {}, {}
    for name in ["x", "ctx_768"] + ["L0_xattn_" + n for n in _WEIGHTS]:
        a = _np.ascontiguousarray(inputs[name])
        arrays[f"in_{name}_dram"] = a
        aps[name] = nc.dram_tensor(f"in_{name}_dram", a.shape, _mybir.dt.from_np(a.dtype), kind="ExternalInput").ap()
    out = nc.dram_tensor("out_0_dram", (B, N, D), _mybir.dt.float32, kind="ExternalOutput").ap()
    layer(nc, aps["x"], aps["ctx_768"], {n: aps["L0_xattn_" + n] for n in _WEIGHTS}, out)
    r = _run(nc, [arrays], core_ids=[0])
    return r.results[0]["out_0_dram"]
```
